# Optimizing a Trainium2 kernel written in Bass

```python
import numpy as np
import jax
import jax.numpy as jnp

def _softmax(x, axis=-1):
    return jax.nn.softmax(x, axis=axis)

def _gelu(x):
    return jax.nn.gelu(x, approximate=True)

def _silu(x):
    return jax.nn.silu(x)

def _sigmoid(x):
    return jax.nn.sigmoid(x)

def _layernorm(x, axis=-1, eps=1e-05):
    m = jnp.mean(x, axis=axis, keepdims=True)
    v = jnp.var(x, axis=axis, keepdims=True)
    return (x - m) / jnp.sqrt(v + eps)

def _scatter_add(tgt, idx, src, axis=0):
    return tgt.at[idx].add(src)

def _segment_sum(src, seg, n):
    return jax.ops.segment_sum(src, seg, n)
kernel_name = 'mk_conv_attn_hybrid_d2_conv_nchw256_r4_12e807'

def setup_inputs(seed: int=0):
    np.random.seed(seed)
    _w = jnp.asarray

    def _rec_inputs():
        import jax
        import jax.numpy as jnp
        _gk = jax.random.key(seed)
        x = -0.0002928 + 1 * jax.random.normal(jax.random.fold_in(_gk, 1), (4, 64, 16, 16), jnp.float32)
        return x
    x = _rec_inputs()

    def _L0_conv_setup():
        import jax, jax.numpy as jnp
        import numpy as np
        K = 7
        GC = 16
        BN_EPS = 1e-05
        key = jax.random.key(seed)
        ks = jax.random.split(key, 9)
        B, C, H, W = (4, 64, 16, 16)
        OUT = 64
        CR = C // 4
        G = C // GC
        x = jax.random.normal(ks[0], (B, C, H, W), dtype=jnp.float32)
        w1 = jax.random.normal(ks[1], (CR, C), dtype=jnp.float32) * (1.0 / np.sqrt(C))
        gamma = jax.random.uniform(ks[2], (CR,), dtype=jnp.float32, minval=0.5, maxval=1.5)
        beta = jax.random.normal(ks[3], (CR,), dtype=jnp.float32) * 0.1
        mean = jax.random.normal(ks[4], (CR,), dtype=jnp.float32) * 0.1
        var = jax.random.uniform(ks[5], (CR,), dtype=jnp.float32, minval=0.5, maxval=1.5)
        w2 = jax.random.normal(ks[6], (K * K * G, CR), dtype=jnp.float32) * (1.0 / np.sqrt(CR))
        b2 = jax.random.normal(ks[7], (K * K * G,), dtype=jnp.float32) * 0.01
        wp = jax.random.normal(ks[8], (OUT, C), dtype=jnp.float32) * (1.0 / np.sqrt(C))
        return {'x': x, 'w1': w1, 'gamma': gamma, 'beta': beta, 'mean': mean, 'var': var, 'w2': w2, 'b2': b2, 'wp': wp}
    _L0_conv_all = _L0_conv_setup()
    _L0_conv_in = {k: v for k, v in _L0_conv_all.items() if k in ('w1', 'gamma', 'beta', 'mean', 'var', 'w2', 'b2', 'wp')}
    del _L0_conv_all

    def _L1_attn_setup():
        import jax, jax.numpy as jnp
        import numpy as np
        B, N, C, H = (2, 2048, 64, 8)
        EPS = 1e-05
        key = jax.random.key(seed)
        k1, k2, k3, k4, k5 = jax.random.split(key, 5)
        s = 1.0 / np.sqrt(C)
        return {'emb': jax.random.normal(k1, (B, N, C), dtype=jnp.float32), 'Wq': jax.random.normal(k2, (C, C * H), dtype=jnp.float32) * s, 'Wk': jax.random.normal(k3, (C, C * H), dtype=jnp.float32) * s, 'Wv': jax.random.normal(k4, (C, C * H), dtype=jnp.float32) * s, 'Wo': jax.random.normal(k5, (C * H, C), dtype=jnp.float32) * s}
    _L1_attn_all = _L1_attn_setup()
    _L1_attn_in = {k: v for k, v in _L1_attn_all.items() if k in ('Wq', 'Wk', 'Wv', 'Wo')}
    del _L1_attn_all

    def _L1_ffn_setup():
        import math
        import jax, jax.numpy as jnp
        import numpy as np
        CAPACITY_FACTOR = 1.25
        TOP_K = 2
        LN_EPS = 1e-05

        def _layer_norm(x, gamma, beta):
            mu = jnp.mean(x, axis=-1, keepdims=True)
            var = jnp.var(x, axis=-1, keepdims=True)
            return (x - mu) * jax.lax.rsqrt(var + LN_EPS) * gamma + beta
        key = jax.random.key(seed)
        ks = jax.random.split(key, 4)
        B, S, D, F, E = (8, 1024, 64, 128, 8)
        x = jax.random.normal(ks[0], (B, S, D), dtype=jnp.float32)
        Wr = jax.random.normal(ks[1], (D, E), dtype=jnp.float32) / np.sqrt(D)
        br = jnp.zeros((E,), jnp.float32)
        W1 = jax.random.normal(ks[2], (E, D, F), dtype=jnp.float32) / np.sqrt(D)
        b1 = jnp.zeros((E, F), jnp.float32)
        W2 = jax.random.normal(ks[3], (E, F, D), dtype=jnp.float32) / np.sqrt(F)
        b2 = jnp.zeros((E, D), jnp.float32)
        gamma = jnp.ones((D,), jnp.float32)
        beta = jnp.zeros((D,), jnp.float32)
        return {'x': x, 'Wr': Wr, 'br': br, 'W1': W1, 'b1': b1, 'W2': W2, 'b2': b2, 'gamma': gamma, 'beta': beta}
    _L1_ffn_all = _L1_ffn_setup()
    _L1_ffn_in = {k: v for k, v in _L1_ffn_all.items() if k in ('Wr', 'br', 'W1', 'b1', 'W2', 'b2', 'gamma', 'beta')}
    del _L1_ffn_all
    return {'x': x, 'L0_conv_w1': _L0_conv_in['w1'], 'L0_conv_gamma': _L0_conv_in['gamma'], 'L0_conv_beta': _L0_conv_in['beta'], 'L0_conv_mean': _L0_conv_in['mean'], 'L0_conv_var': _L0_conv_in['var'], 'L0_conv_w2': _L0_conv_in['w2'], 'L0_conv_b2': _L0_conv_in['b2'], 'L0_conv_wp': _L0_conv_in['wp'], 'L1_attn_Wq': _L1_attn_in['Wq'], 'L1_attn_Wk': _L1_attn_in['Wk'], 'L1_attn_Wv': _L1_attn_in['Wv'], 'L1_attn_Wo': _L1_attn_in['Wo'], 'L1_ffn_Wr': _L1_ffn_in['Wr'], 'L1_ffn_br': _L1_ffn_in['br'], 'L1_ffn_W1': _L1_ffn_in['W1'], 'L1_ffn_b1': _L1_ffn_in['b1'], 'L1_ffn_W2': _L1_ffn_in['W2'], 'L1_ffn_b2': _L1_ffn_in['b2'], 'L1_ffn_gamma': _L1_ffn_in['gamma'], 'L1_ffn_beta': _L1_ffn_in['beta']}

def reference(x, L0_conv_w1, L0_conv_gamma, L0_conv_beta, L0_conv_mean, L0_conv_var, L0_conv_w2, L0_conv_b2, L0_conv_wp, L1_attn_Wq, L1_attn_Wk, L1_attn_Wv, L1_attn_Wo, L1_ffn_Wr, L1_ffn_br, L1_ffn_W1, L1_ffn_b1, L1_ffn_W2, L1_ffn_b2, L1_ffn_gamma, L1_ffn_beta):
    import jax
    import jax.numpy as jnp

    def _L0_conv_ref(x, w1, gamma, beta, mean, var, w2, b2, wp):
        import jax, jax.numpy as jnp
        import numpy as np
        K = 7
        GC = 16
        BN_EPS = 1e-05
        b, c, h, w = x.shape
        groups = c // GC
        y = jnp.einsum('oc,bchw->bohw', w1, x)
        scale = (gamma * jax.lax.rsqrt(var + BN_EPS))[None, :, None, None]
        y = jax.nn.relu((y - mean[None, :, None, None]) * scale + beta[None, :, None, None])
        wt = jnp.einsum('oc,bchw->bohw', w2, y) + b2[None, :, None, None]
        wt = wt.reshape(b, groups, 1, K * K, h, w)
        p = (K - 1) // 2
        patches = jax.lax.conv_general_dilated_patches(x, (K, K), (1, 1), ((p, p), (p, p)))
        patches = patches.reshape(b, groups, GC, K * K, h, w)
        out = (wt * patches).sum(axis=3).reshape(b, c, h, w)
        return jnp.einsum('oc,bchw->bohw', wp, out)

    def _L1_attn_ref(emb, Wq, Wk, Wv, Wo):
        import jax, jax.numpy as jnp
        import numpy as np
        B, N, C, H = (2, 2048, 64, 8)
        EPS = 1e-05
        b, n, c = emb.shape
        h = Wq.shape[1] // c

        def heads(x):
            return x.reshape(b, n, h, c).transpose(0, 2, 1, 3)
        qh = heads(emb @ Wq)
        kh = heads(emb @ Wk)
        vh = heads(emb @ Wv)
        attn = jnp.einsum('bhnd,bhne->bhde', qh, kh)
        mu = attn.mean(axis=(2, 3), keepdims=True)
        var = attn.var(axis=(2, 3), keepdims=True)
        attn = (attn - mu) * jax.lax.rsqrt(var + EPS)
        attn = jax.nn.softmax(attn, axis=3)
        ctx = jnp.einsum('bhde,bhne->bhdn', attn, vh)
        ctx = ctx.transpose(0, 3, 2, 1).reshape(b, n, c * h)
        return ctx @ Wo

    def _L1_ffn_ref(x, Wr, br, W1, b1, W2, b2, gamma, beta):
        import math
        import jax, jax.numpy as jnp
        import numpy as np
        CAPACITY_FACTOR = 1.25
        TOP_K = 2
        LN_EPS = 1e-05

        def _layer_norm(x, gamma, beta):
            mu = jnp.mean(x, axis=-1, keepdims=True)
            var = jnp.var(x, axis=-1, keepdims=True)
            return (x - mu) * jax.lax.rsqrt(var + LN_EPS) * gamma + beta
        B, S, D = x.shape
        E = Wr.shape[1]
        N = B * S
        K = TOP_K
        logits = jnp.mean(x, axis=1) @ Wr + br
        routing_weights = jax.nn.softmax(logits, axis=-1)
        capacity = float(math.ceil(N * CAPACITY_FACTOR / E))
        expected_loads = routing_weights.sum(axis=0) * (N / B)
        scale = jnp.where(expected_loads > capacity, capacity / expected_loads, 1.0)
        routing_weights = jax.nn.softmax(routing_weights * scale, axis=-1)
        rw_tok = jnp.broadcast_to(routing_weights[:, None, :], (B, S, E)).reshape(N, E)
        top_w, top_i = jax.lax.top_k(rw_tok, K)
        top_w = jax.nn.softmax(top_w, axis=-1)
        xf = x.reshape(N, D)
        h = jax.nn.gelu(jnp.einsum('nd,edf->enf', xf, W1) + b1[:, None, :], approximate=False)
        y = jnp.einsum('enf,efd->end', h, W2) + b2[:, None, :]
        w_dense = jnp.zeros((N, E), x.dtype).at[jnp.arange(N)[:, None], top_i].add(top_w)
        out = jnp.einsum('ne,end->nd', w_dense, y).reshape(B, S, D)
        out = _layer_norm(out + x, gamma, beta)
        return out

    def _gn(v, G=32, eps=1e-05):
        B_, C_, H_, W_ = v.shape
        g = v.reshape(B_, G, C_ // G, H_, W_)
        m = jnp.mean(g, axis=(2, 3, 4), keepdims=True)
        s = jnp.var(g, axis=(2, 3, 4), keepdims=True)
        return ((g - m) / jnp.sqrt(s + eps)).reshape(v.shape)

    def _ln_c(v, eps=1e-06):
        m = jnp.mean(v, axis=1, keepdims=True)
        s = jnp.var(v, axis=1, keepdims=True)
        return (v - m) / jnp.sqrt(s + eps)

    def _ln_t(v, eps=1e-05):
        m = jnp.mean(v, axis=-1, keepdims=True)
        s = jnp.var(v, axis=-1, keepdims=True)
        return (v - m) / jnp.sqrt(s + eps)

    def _to_tokens(v):
        B_, C_, H_, W_ = v.shape
        return v.reshape(B_, C_, H_ * W_).transpose(0, 2, 1)

    def _from_tokens(t, like):
        B_, C_, H_, W_ = like.shape
        return t.transpose(0, 2, 1).reshape(B_, C_, H_, W_)
    x = x + _L0_conv_ref(_gn(x), L0_conv_w1, L0_conv_gamma, L0_conv_beta, L0_conv_mean, L0_conv_var, L0_conv_w2, L0_conv_b2, L0_conv_wp)
    t = _to_tokens(x)
    t = t + _L1_attn_ref(_ln_t(t), L1_attn_Wq, L1_attn_Wk, L1_attn_Wv, L1_attn_Wo)
    t = t + _L1_ffn_ref(_ln_t(t), L1_ffn_Wr, L1_ffn_br, L1_ffn_W1, L1_ffn_b1, L1_ffn_W2, L1_ffn_b2, L1_ffn_gamma, L1_ffn_beta)
    x = _from_tokens(t, x)
    return x

_drawn_inputs = setup_inputs


def setup_inputs(seed=0):
    import zlib

    import numpy as np

    out = dict(_drawn_inputs(seed))
    spreads = {'L1_ffn_br': (0.0, 0.1),
     'L1_ffn_b1': (0.0, 0.8),
     'L1_ffn_b2': (0.0, 0.745),
     'L1_ffn_gamma': (1.0, 0.2),
     'L1_ffn_beta': (0.0, 0.489)}
    factors = {'L0_conv_b2': 4.228}
    for name, (base, spread) in spreads.items():
        noise = np.random.default_rng([zlib.crc32(name.encode()), seed]).standard_normal(out[name].shape)
        drawn = base * np.exp(spread * noise) if base else spread * noise
        out[name] = jnp.asarray(drawn.astype(out[name].dtype))
    for name, factor in factors.items():
        out[name] = (out[name] * factor).astype(out[name].dtype)
    return out
```

```python
from contextlib import ExitStack

import concourse.bass as bass
from concourse import mybir

F32 = mybir.dt.float32
I32 = mybir.dt.int32
U32 = mybir.dt.uint32
ALU = mybir.AluOpType
ACT = mybir.ActivationFunctionType
AX = mybir.AxisListType

P = 128
B, C, H, W = 4, 64, 16, 16
HW = H * W
BH = B // 2
TOK = P
NS = HW // TOK
NT = BH * NS * 2
K = 7
PAD = K // 2
GC = 16
G = C // GC
CR = C // 4
WIN = K * W
TAPS = P
EDGES = [*range(PAD), *range(W - PAD, W)]
HEADS = 8
EXP = 8
FF = 128
TOPK = 2
CAPACITY = -(-B * HW * 5 // (4 * EXP))
EPS = 1e-5
BANK = 512
NBANK = 8

CHUNKS = [
    ("w1T", "V"), ("w2T", "A"), ("bn", "V"), ("gn", "V"), ("y0", "A"), ("y1", "A"),
    ("x0", "V"), ("x1", "V"), ("x2", "V"), ("x3", "A"), ("x4", "V"), ("x5", "A"), ("x6", "V"), ("x7", "A"),
    ("wpT", "A"),
    ("w0", "V"), ("w1", "A"), ("w2", "V"), ("w3", "A"), ("w4", "V"), ("w5", "A"), ("w6", "V"), ("w7", "A"),
    ("d0", "V"), ("d1", "A"), ("d2", "V"), ("d3", "A"),
    ("t0", "A"), ("t1", "A"), ("t2", "A"), ("t3", "A"),
    ("wvT", "A"), ("b1T", "A"),
    ("gram", "V"), ("eT", "A"), ("gk0", "V"), ("gk1", "A"), ("attn0", "A"), ("attn1", "A"), ("astat", "V"),
    ("z0", "V"), ("z1", "A"), ("m", "V"), ("o", "V"),
    ("t2T", "A"), ("fT", "A"), ("logits", "V"),
    ("h0", "A"), ("h1", "A"), ("h2", "A"), ("h3", "A"), ("h4", "A"), ("h5", "A"), ("h6", "A"), ("h7", "A"),
    ("ffn", "V"), ("nT", "V"),
]
INDEX = {name: j for j, (name, _) in enumerate(CHUNKS)}


def reads_until(j):
    return sum(1 for _, r in CHUNKS[:j + 1] if r == CHUNKS[j][1])


def build(nc, d, out):
    with ExitStack() as ctx:
        def sb(name, shape, dt=F32):
            return ctx.enter_context(nc.sbuf_tensor(name, shape, dt))

        def sem(name):
            return ctx.enter_context(nc.semaphore(name))

        ident = sb("ident", [P, P])
        pair = sb("pair", [P, P])
        rep = sb("rep", [32, G, 32])
        gmask = sb("gmask", [P, 2 * G])
        blk = sb("blk", [P, P])
        mean_t = sb("mean_t", [P, P])
        w1 = sb("w1", [CR, C])
        bnv = sb("bnv", [CR, 4])
        bn_ab = sb("bn_ab", [CR + 1, 2])
        bn_t = sb("bn_t", [CR, 4])
        w2l = sb("w2l", [K * K, G, 32])
        wp = sb("wp", [C, C])
        wpT = sb("wpT", [P, C])
        wpg = sb("wpg", [P, G, 2, C])
        wq = sb("wq", [P, HEADS, 2, C])
        wk = sb("wk", [P, HEADS * C])
        wv = sb("wv", [C, HEADS * C])
        wvT = sb("wvT", [P, HEADS // 2, C])
        wo = sb("wo", [P, HEADS, C])
        wr = sb("wr", [P, 2, EXP])
        br = sb("br", [P, EXP])
        fw1 = sb("fw1", [P, EXP, FF])
        fw2 = sb("fw2", [P, EXP, C])
        fb1 = sb("fb1", [EXP, FF])
        fb1T = sb("fb1T", [P, EXP])
        fb2 = sb("fb2", [P, EXP, C])
        gb = sb("gb", [P, 2])
        x = sb("x", [P, BH, HW])
        xp = sb("xp", [P, BH, H + 2 * PAD, W])
        gst = sb("gst", [P, BH, 6])
        gmv = sb("gmv", [P, BH, 2])
        gm2 = sb("gm2", [P, BH])
        gs = sb("gs", [P, BH, 2])
        gr = sb("gr", [P, BH])
        w1T = sb("w1T", [P, G * 32])
        taps = sb("taps", [P, 1 + len(EDGES), TAPS])
        bns = sb("bns", [P, 2])
        y = sb("y", [P, W, 2, BH, H])
        xw = sb("xw", [WIN, BH, H, P])
        wt = sb("wt", [WIN, 2, BH, H, G, W])
        dsb = sb("dsb", [P, G, BH, H, W])
        t = sb("t", [P, NT, C])
        e = sb("e", [P, NT, C])
        eT = sb("eT", [P, BH, HW])
        gram = sb("gram", [P, BH, P])
        gk = sb("gk", [P, BH, HEADS, C])
        a = sb("a", [P, HEADS, BH, C])
        ac = sb("ac", [P, HEADS, BH, C])
        asq = sb("asq", [P, HEADS, BH, C])
        amax = sb("amax", [P, HEADS, BH])
        ast = sb("ast", [P, 2, HEADS, BH])
        asc = sb("asc", [P, 2, HEADS, BH])
        ar = sb("ar", [P, HEADS, BH])
        prob = sb("prob", [P, HEADS, BH, C])
        rsum = sb("rsum", [P, HEADS, BH])
        wos = sb("wos", [P, HEADS, BH, C])
        z = sb("z", [P, 2, HEADS // 2, BH, C])
        m = sb("m", [P, BH, 2, C])
        t2 = sb("t2", [P, NT, C])
        t2T = sb("t2T", [P, BH, HW])
        f = sb("f", [P, NT, C])
        fT = sb("fT", [P, BH, HW])
        fsum = sb("fsum", [P, BH])
        rl = sb("rl", [P, BH, 2, EXP])
        rt = sb("rt", [P, 4, B, EXP])
        rs = sb("rs", [P, 8, EXP])
        top = sb("top", [P, B, 8])
        topi = sb("topi", [P, B, 8], U32)
        gate = sb("gate", [P, B, TOPK])
        w1s = sb("w1s", [P, BH, TOPK, FF])
        b1s = sb("b1s", [P, B, TOPK])
        w2s = sb("w2s", [P, B, TOPK, C])
        b2s = sb("b2s", [P, B, C])
        h = sb("h", [P, B, TOPK, HW])
        fb = sb("fb", [P, NT, C])
        u = sb("u", [P, NT, C])
        n = sb("n", [P, NT, C])
        res = sb("res", [P, BH, HW])
        lst = sb("lst", [P, NT, 6])
        lt = sb("lt", [P, 6, NT])
        rq = sb("rq", [P, 2, 2 * HEADS])

        ps = ctx.enter_context(nc.psum_tensor("ps", [P, NBANK, BANK], F32))

        def bank(name):
            return ps[:, INDEX[name] % NBANK, :]

        written = sem("psum_written")
        read_v = sem("psum_read_by_vector")
        read_a = sem("psum_read_by_scalar")
        v_seq = sem("vector_steps")
        g_seq = sem("gpsimd_steps")
        a_seq = sem("scalar_steps")
        dma = {k: sem("loaded_" + k) for k in ("x", "w1", "bn", "w2", "wp", "wq", "wk", "wv", "wo", "wr", "w_ffn", "fb")}
        stored = sem("stored")
        const = {k: sem("made_" + k) for k in ("rep", "w2l", "ident", "pair", "gmask", "wq", "wr", "taps", "gram", "m",
                                               "xp", "blk", "mean", "wpg", "bnab")}
        made = {k: sem("sb_" + k) for k in (
            "w1T", "taps", "bns", "bnab", "gmv", "xn", "wpT", "e", "e_v", "gram", "c", "cr", "ast", "m", "t2", "f", "rl", "logit", "exp1",
            "logit2", "exp2", "dtop", "etop", "gate", "topi", "w1s", "b1s", "w2s", "n", "res", "a", "asq", "amax", "prob",
            "rr", "wos_g", "wos_v", "beta", "fsum", "t", "ar")}
        block = ctx.enter_context(nc.Block())

        def tap_view(v, lo, hi):
            at = W - 1 - PAD
            return taps[:, v, at:at + WIN].rearrange("p (i j) -> p i j", j=W)[:, :, lo:hi]

        def wait_chunk(eng, name):
            eng.wait_ge(written, INDEX[name] + 1)

        def wait_read(eng, name):
            j = INDEX[name]
            eng.wait_ge(read_v if CHUNKS[j][1] == "V" else read_a, reads_until(j))

        def involution_reads(eng, copy, who, read):
            for name, reader in CHUNKS[INDEX["x0"]:INDEX["d3"] + 1]:
                if reader != who:
                    continue
                wait_chunk(eng, name)
                src = bank(name)
                if name == "wpT":
                    copy(wpT[:, :], src[:, 0:C]).then_inc(read, 1)
                    continue
                i = int(name[1:])
                if name[0] == "x":
                    t_, r = divmod(4 * i, H)
                    copy(xw[:, t_, r:r + 4, :], src[0:WIN, :].rearrange("p (r q) -> p r q", r=4)).then_inc(read, 1)
                elif name[0] == "w":
                    g, w0 = i % G, 8 * (i // G)
                    copy(wt[:, :, :, :, g, w0:w0 + 8].rearrange("p l t h w -> p (l t h) w"),
                         src[0:WIN, :].rearrange("p (w q) -> p q w", w=8)).then_inc(read, 1)
                else:
                    t_, s = divmod(i, NS)
                    copy(dsb[:, :, t_, 8 * s:8 * s + 8, :].rearrange("p g h w -> p h g w"),
                         src.rearrange("p (h g w) -> p h g w", h=8, g=G)).then_inc(read, 1)

        @block.sync
        def _(sp):
            sp.dma_start(x[:, :, :], d["x"].rearrange("(t u) c h w -> (u c) t (h w)", t=BH)).then_inc(dma["x"], 16)
            sp.dma_start(w1[:, :], d["L0_conv_w1"]).then_inc(dma["w1"], 16)
            sp.wait_ge(const["w2l"], 1)
            sp.dma_start(w2l[:, :, 0:CR], d["L0_conv_w2"].rearrange("(g k) c -> k g c", g=G)).then_inc(dma["w2"], 16)
            sp.dma_start(w2l[:, :, CR:CR + 1], d["L0_conv_b2"].rearrange("(g k o) -> k g o", g=G, o=1), allow_slow_non_contiguous=True).then_inc(dma["w2"], 16)
            for l in range(2):
                sp.dma_start(wk[l * C:(l + 1) * C, :], d["L1_attn_Wk"]).then_inc(dma["wk"], 16)
            sp.wait_ge(const["wq"], 1)
            for l in range(2):
                sp.dma_start(wq[l * C:(l + 1) * C, :, l, :], d["L1_attn_Wq"].rearrange("c (h e) -> c h e", h=HEADS)).then_inc(dma["wq"], 16)
            sp.dma_start(wv[:, :], d["L1_attn_Wv"]).then_inc(dma["wv"], 16)
            for l in range(2):
                sp.dma_start(wo[l * C:(l + 1) * C, :, :], d["L1_attn_Wo"].rearrange("(e h) j -> e h j", h=HEADS)).then_inc(dma["wo"], 16)
            for l in range(2):
                sp.dma_start(fw1[l * C:(l + 1) * C, :, :], d["L1_ffn_W1"].rearrange("e c f -> c e f")).then_inc(dma["w_ffn"], 16)
            sp.dma_start(fw2[:, :, :], d["L1_ffn_W2"].rearrange("e f j -> f e j")).then_inc(dma["w_ffn"], 16)
            for i in range(BH):
                sp.wait_ge(made["res"], i + 1)
                sp.dma_start(out.rearrange("(t u) c h w -> (u c) t (h w)", t=BH)[:, i, :], res[:, i, :]).then_inc(stored, 16)
            sp.wait_ge(stored, 16 * BH)

        @block.gpsimd
        def _(pool):
            steps = [0]

            def link(ins):
                steps[0] += 1
                ins.then_inc(g_seq, 1)
                pool.wait_ge(g_seq, steps[0])

            def zero(ap, name):
                return pool.memset(ap, 0.0).then_inc(const[name], 1)

            zero(w2l[:, :, :], "w2l")
            link(pool.memset(rep[:, :, :], 0.0))
            pool.affine_select(out=rep[:, :, :], in_=rep[:, :, :], compare_op=ALU.not_equal, fill=1.0, base=0,
                               pattern=[[0, G], [-1, 32]], channel_multiplier=1).then_inc(const["rep"], 1)
            link(pool.memset(pair[:, :], 0.5))
            v = pair[:, :].rearrange("p (j u) -> p j u", u=2)
            link(pool.affine_select(out=v, in_=v, compare_op=ALU.is_ge, fill=0.0, base=0, pattern=[[-2, C], [0, 2]], channel_multiplier=1))
            pool.affine_select(out=v, in_=v, compare_op=ALU.is_ge, fill=0.0, base=1, pattern=[[2, C], [0, 2]], channel_multiplier=-1).then_inc(const["pair"], 1)
            link(pool.memset(ident[:, :], 0.0))
            pool.affine_select(out=ident[:, :], in_=ident[:, :], compare_op=ALU.not_equal, fill=1.0, base=0,
                               pattern=[[-1, P]], channel_multiplier=1).then_inc(const["ident"], 1)
            zero(taps[:, :, :], "taps")
            zero(xp[:, :, :, :], "xp")
            zero(wq[:, :, :, :], "wq")
            zero(wr[:, :, :], "wr")
            pool.wait_ge(const["wr"], 1)
            for l in range(2):
                pool.dma_start(wr[l * C:(l + 1) * C, l, :], d["L1_ffn_Wr"]).then_inc(dma["wr"], 16)
            pool.dma_start(br[:, :], d["L1_ffn_br"].rearrange("(o e) -> o e", o=1).broadcast_to([P, EXP])).then_inc(dma["wr"], 16)
            pool.dma_start(fb1[:, :], d["L1_ffn_b1"]).then_inc(dma["fb"], 16)
            pool.dma_start(fb2[:, :, :], d["L1_ffn_b2"].rearrange("(o e) j -> o e j", o=1).broadcast_to([P, EXP, C])).then_inc(dma["fb"], 16)
            for l in range(2):
                pool.dma_start(gb[l * C:(l + 1) * C, 0:1], d["L1_ffn_gamma"].rearrange("(c o) -> c o", o=1)).then_inc(dma["fb"], 16)
                pool.dma_start(gb[l * C:(l + 1) * C, 1:2], d["L1_ffn_beta"].rearrange("(c o) -> c o", o=1)).then_inc(dma["fb"], 16)
            wait_read(pool, "w2T")
            for v, w in enumerate(EDGES):
                lo, hi = max(0, PAD - w), min(K, W + PAD - w)
                pool.tensor_copy(tap_view(v + 1, lo, hi), tap_view(0, lo, hi)).then_inc(made["taps"], 1)
            link(pool.memset(gmask[:, :], 1.0))
            link(pool.affine_select(out=gmask[:, :], in_=gmask[:, :], compare_op=ALU.is_ge, fill=0.0, base=0, pattern=[[-GC, 2 * G]], channel_multiplier=1))
            link(pool.affine_select(out=gmask[:, :], in_=gmask[:, :], compare_op=ALU.is_ge, fill=0.0, base=GC - 1, pattern=[[GC, 2 * G]], channel_multiplier=-1))
            zero(gram[:, :, :], "gram")
            zero(m[:, :, :, :], "m")
            link(pool.memset(wpg[:, :, :, :], 0.0))
            wait_read(pool, "wpT")
            for l in range(2):
                r = slice(l * C, (l + 1) * C)
                pool.tensor_tensor(wpg[r, :, l, :], wpT[r, :].unsqueeze(1).to_broadcast([C, G, C]),
                                   gmask[r, l * G:(l + 1) * G].unsqueeze(2).to_broadcast([C, G, C]), ALU.mult).then_inc(const["wpg"], 1)
                pool.wait_ge(const["wpg"], l + 1)
            link(pool.memset(blk[:, :], 0.0))
            for l in range(2):
                r = slice(l * C, (l + 1) * C)
                pool.memset(blk[r, r], 1.0 / (C * C)).then_inc(const["blk"], 1)
                pool.wait_ge(const["blk"], l + 1)
            pool.memset(mean_t[:, :], 1.0 / HW).then_inc(const["mean"], 1)
            hh = slice(HEADS // 2, HEADS)
            pool.wait_ge(made["amax"], 2)
            pool.tensor_tensor(ac[:, hh, :, :], a[:, hh, :, :], amax[:, hh, :].unsqueeze(3).to_broadcast([P, HEADS // 2, BH, C]), ALU.subtract).then_inc(made["c"], 1)
            pool.wait_ge(made["c"], 1)
            pool.wait_ge(made["ar"], 1)
            pool.tensor_tensor(ac[:, hh, :, :], ac[:, hh, :, :], ar[:, hh, :].unsqueeze(3).to_broadcast([P, HEADS // 2, BH, C]), ALU.mult).then_inc(made["cr"], 1)
            pool.wait_ge(made["rr"], 1)
            pool.wait_ge(dma["wo"], 32)
            pool.tensor_tensor(wos[:, hh, :, :], wo[:, hh, :].unsqueeze(2).to_broadcast([P, HEADS // 2, BH, C]),
                               rsum[:, hh, :].unsqueeze(3).to_broadcast([P, HEADS // 2, BH, C]), ALU.mult).then_inc(made["wos_g"], 1)

        @block.scalar
        def _(act):
            act.dma_start(bnv[:, 0:1], d["L0_conv_gamma"].rearrange("(c o) -> c o", o=1)).then_inc(dma["bn"], 16)
            act.dma_start(bnv[:, 1:2], d["L0_conv_beta"].rearrange("(c o) -> c o", o=1)).then_inc(dma["bn"], 16)
            act.dma_start(bnv[:, 2:3], d["L0_conv_mean"].rearrange("(c o) -> c o", o=1)).then_inc(dma["bn"], 16)
            act.dma_start(bnv[:, 3:4], d["L0_conv_var"].rearrange("(c o) -> c o", o=1)).then_inc(dma["bn"], 16)
            act.dma_start(wp[:, :], d["L0_conv_wp"]).then_inc(dma["wp"], 16)
            act.preload_act_table(ACT.Exp)

            def copy(dst, src):
                return act.activation(dst, src, ACT.Copy)

            act.wait_ge(const["taps"], 1)
            wait_chunk(act, "w2T")
            copy(tap_view(0, 0, K), bank("w2T")[:, 0:K * K].rearrange("p (i j) -> p i j", i=K)).then_inc(read_a, 1)
            act.wait_ge(made["bns"], 1)
            for l in range(2):
                wait_chunk(act, f"y{l}")
                act.activation(y[:, :, l, :, :].rearrange("p w t h -> p t h w"),
                               bank(f"y{l}").rearrange("p (t h w) -> p t h w", t=BH, h=H), ACT.Relu,
                               bias=bns[:, 1:2], scale=bns[:, 0:1]).then_inc(read_a, 1)
            involution_reads(act, copy, "A", read_a)

            for i in range(4):
                wait_chunk(act, f"t{i}")
                copy(t[:, 2 * i:2 * i + 2, :], bank(f"t{i}")[:, 0:P]).then_inc(read_a, 1)
            wait_chunk(act, "wvT")
            copy(wvT[:, :, :], bank("wvT")[:, 0:HEADS // 2 * C]).then_inc(read_a, 1)
            wait_chunk(act, "b1T")
            copy(fb1T[:, :], bank("b1T")[:, 0:EXP]).then_inc(read_a, 1)
            wait_chunk(act, "eT")
            copy(eT[:, :, :], bank("eT")).then_inc(read_a, 1)
            wait_chunk(act, "gk1")
            copy(gk[:, 1, :, :], bank("gk1")).then_inc(read_a, 1)
            for i in range(2):
                hs = slice(i * HEADS // 2, (i + 1) * HEADS // 2)
                wait_chunk(act, f"attn{i}")
                copy(a[:, hs, :, :], bank(f"attn{i}")).then_inc(read_a, 1)
            for i in range(2):
                hs = slice(i * HEADS // 2, (i + 1) * HEADS // 2)
                act.wait_ge(read_a, reads_until(INDEX[f"attn{i}"]))
                act.activation(asq[:, hs, :, :], a[:, hs, :, :], ACT.Square).then_inc(made["asq"], 1)
            act.wait_ge(made["ast"], 1)
            hs = slice(0, HEADS // 2)
            act.activation(prob[:, hs, :, :], ac[:, hs, :, :], ACT.Exp).then_inc(made["prob"], 1)
            act.wait_ge(made["cr"], 1)
            hs = slice(HEADS // 2, HEADS)
            act.activation(prob[:, hs, :, :], ac[:, hs, :, :], ACT.Exp).then_inc(made["prob"], 1)
            wait_chunk(act, "z1")
            copy(z[:, 1, :, :, :], bank("z1")).then_inc(read_a, 1)
            act.wait_ge(dma["fb"], 16 * 6)
            wait_chunk(act, "t2T")
            act.activation(t2T[:, :, :], bank("t2T"), ACT.Identity, bias=gb[:, 1:2]).then_inc(read_a, 1)
            wait_chunk(act, "fT")
            for i in range(BH):
                last = act.activation(fT[:, i, :], bank("fT")[:, i * HW:(i + 1) * HW], ACT.Copy, accum_out=fsum[:, i:i + 1])
                last.then_inc(made["fsum"], 1)
            act.wait_ge(made["fsum"], 2)
            act.nop().then_inc(read_a, 1)
            act.wait_ge(made["logit"], 1)
            act.activation(rt[:, 1, :, :], rt[:, 0, :, :], ACT.Exp).then_inc(made["exp1"], 1)
            act.wait_ge(made["logit2"], 1)
            act.activation(rt[:, 1, :, :], rt[:, 0, :, :], ACT.Exp).then_inc(made["exp2"], 1)
            act.wait_ge(made["dtop"], 1)
            act.activation(gate[:, :, 1:2], rs[:, 5, 0:B].unsqueeze(2), ACT.Exp).then_inc(made["etop"], 1)
            act.preload_act_table(ACT.Gelu)
            act.wait_ge(made["b1s"], 1)
            for i in range(B * TOPK):
                b, k = divmod(i, TOPK)
                wait_chunk(act, f"h{i}")
                act.activation(h[:, b, k, :], bank(f"h{i}")[:, 0:HW], ACT.Gelu, bias=b1s[:, b, k:k + 1]).then_inc(read_a, 1)

        @block.vector
        def _(dve):
            steps = [0]

            def link(ins):
                steps[0] += 1
                ins.then_inc(v_seq, 1)
                dve.wait_ge(v_seq, steps[0])

            def rsqrt(r, v, tmp):
                link(dve.tensor_scalar(r.bitcast(I32), v.bitcast(I32), -0.5, float(0x5F3759DF), ALU.mult, ALU.add))
                for _ in range(3):
                    link(dve.tensor_tensor(tmp, r, r, ALU.mult))
                    link(dve.scalar_tensor_tensor(tmp, tmp, -0.5, v, ALU.mult, ALU.mult))
                    link(dve.scalar_tensor_tensor(r, tmp, 1.5, r, ALU.add, ALU.mult))

            def layer_norm(dst, src, done):
                for i in range(NT):
                    ins = dve.bn_stats(lst[:, i, :], src[:, i, :])
                    if i == NT - 1:
                        link(ins)
                me, qe, mo, qo = lst[:, :, 1], lst[:, :, 2], lst[:, :, 4], lst[:, :, 5]
                s, dd, q, v, tmp, r = (lt[:, i, :] for i in range(6))
                dve.tensor_tensor(s, me, mo, ALU.add)
                link(dve.tensor_tensor(dd, me, mo, ALU.subtract))
                dve.tensor_tensor(q, qe, qo, ALU.add)
                link(dve.tensor_tensor(dd, dd, dd, ALU.mult))
                link(dve.scalar_tensor_tensor(q, dd, C / 4.0, q, ALU.mult, ALU.add))
                link(dve.tensor_scalar(v, q, 1.0 / C, EPS, ALU.mult, ALU.add))
                rsqrt(r, v, tmp)
                link(dve.scalar_tensor_tensor(s, s, -0.5, r, ALU.mult, ALU.mult))
                for i in range(NT):
                    ins = dve.tensor_scalar(dst[:, i, :], src[:, i, :], r[:, i:i + 1], s[:, i:i + 1], ALU.mult, ALU.add)
                    if i == NT - 1:
                        ins.then_inc(done, 1)

            dve.wait_ge(dma["x"], 16)
            for i in range(BH):
                ins = dve.bn_stats(gst[:, i, :], x[:, i, :])
            link(ins)
            for i in range(BH):
                ins = dve.bn_aggr(gmv[:, i, :], gst[:, i, :])
            link(ins)
            link(dve.tensor_tensor(gm2[:, :], gmv[:, :, 0], gmv[:, :, 0], ALU.mult))
            dve.tensor_tensor(gmv[:, :, 1], gmv[:, :, 1], gm2[:, :], ALU.add).then_inc(made["gmv"], 1)
            wait_chunk(dve, "w1T")
            dve.tensor_copy(w1T[:, :], bank("w1T")[:, 0:G * 32]).then_inc(read_v, 1)
            dve.memset(bn_ab[:, 0:1], 0.0)
            dve.memset(bn_ab[:, 1:2], 1.0)
            dve.wait_ge(dma["bn"], 64)
            link(dve.tensor_scalar(bn_t[:, 0:1], bnv[:, 3:4], EPS, None, ALU.add))
            rsqrt(bn_t[:, 1:2], bn_t[:, 0:1], bn_t[:, 2:3])
            link(dve.tensor_tensor(bn_ab[0:CR, 0:1], bnv[:, 0:1], bn_t[:, 1:2], ALU.mult))
            link(dve.tensor_tensor(bn_t[:, 3:4], bnv[:, 2:3], bn_ab[0:CR, 0:1], ALU.mult))
            dve.tensor_tensor(bn_ab[0:CR, 1:2], bnv[:, 1:2], bn_t[:, 3:4], ALU.subtract).then_inc(made["bnab"], 1)
            wait_chunk(dve, "bn")
            dve.tensor_copy(bns[:, :], bank("bn")[:, 0:2]).then_inc(made["bns"], 1)
            dve.wait_ge(made["bns"], 1)
            dve.sem_inc(read_v, 1)
            wait_chunk(dve, "gn")
            dve.tensor_copy(gs[:, :, :], bank("gn")[:, 0:2 * BH]).then_inc(read_v, 1)
            dve.wait_ge(read_v, reads_until(INDEX["gn"]))
            link(dve.tensor_tensor(gm2[:, :], gs[:, :, 0], gs[:, :, 0], ALU.mult))
            link(dve.scalar_tensor_tensor(gm2[:, :], gs[:, :, 1], EPS, gm2[:, :], ALU.add, ALU.subtract))
            rsqrt(gr[:, :], gm2[:, :], gs[:, :, 1])
            dve.wait_ge(const["xp"], 1)
            for i in range(BH):
                dve.tensor_scalar(xp[:, i, PAD:PAD + H, :], x[:, i, :].rearrange("p (h w) -> p h w", h=H),
                                  gs[:, i, 0:1], gr[:, i:i + 1], ALU.subtract, ALU.mult).then_inc(made["xn"], 1)
            involution_reads(dve, dve.tensor_copy, "V", read_v)

            wait_read(dve, "t3")
            layer_norm(e, t, made["e"])
            dve.wait_ge(const["gram"], 1)
            wait_chunk(dve, "gram")
            gr_ps = bank("gram")[:, 0:BH * P].rearrange("p (t q) -> p t q", t=BH)
            for l in range(2):
                r = slice(l * C, (l + 1) * C)
                ins = dve.tensor_copy(gram[r, :, r], gr_ps[r, :, r])
            ins.then_inc(read_v, 1)
            wait_chunk(dve, "gk0")
            dve.tensor_copy(gk[:, 0, :, :], bank("gk0")).then_inc(read_v, 1)
            for i in range(2):
                hs = slice(i * HEADS // 2, (i + 1) * HEADS // 2)
                wait_read(dve, f"attn{i}")
                dve.reduce_max(amax[:, hs, :], a[:, hs, :, :], AX.X).then_inc(made["amax"], 1)
                dve.reduce_sum(ast[:, 0, hs, :], a[:, hs, :, :], AX.X)
            for i in range(2):
                hs = slice(i * HEADS // 2, (i + 1) * HEADS // 2)
                dve.wait_ge(made["asq"], i + 1)
                ins = dve.reduce_sum(ast[:, 1, hs, :], asq[:, hs, :, :], AX.X)
            ins.then_inc(made["a"], 1)
            hs = slice(0, HEADS // 2)
            dve.wait_ge(made["amax"], 1)
            link(dve.tensor_tensor(ac[:, hs, :, :], a[:, hs, :, :], amax[:, hs, :].unsqueeze(3).to_broadcast([P, HEADS // 2, BH, C]), ALU.subtract))
            wait_chunk(dve, "astat")
            dve.tensor_copy(asc[:, :, :, :], bank("astat")[:, 0:4 * HEADS]).then_inc(read_v, 1)
            dve.wait_ge(read_v, reads_until(INDEX["astat"]))
            mu, v = asc[:, 0, :, :].rearrange("p h t -> p (h t)"), asc[:, 1, :, :].rearrange("p h t -> p (h t)")
            link(dve.tensor_tensor(mu, mu, mu, ALU.mult))
            link(dve.scalar_tensor_tensor(v, v, EPS, mu, ALU.add, ALU.subtract))
            rsqrt(ar[:, :, :].rearrange("p h t -> p (h t)"), v, rq[:, 0, :])
            dve.tensor_tensor(ac[:, hs, :, :], ac[:, hs, :, :], ar[:, hs, :].unsqueeze(3).to_broadcast([P, HEADS // 2, BH, C]), ALU.mult).then_inc(made["ast"], 1)
            dve.sem_inc(made["ar"], 1)
            for i in range(2):
                hs = slice(i * HEADS // 2, (i + 1) * HEADS // 2)
                dve.wait_ge(made["prob"], i + 1)
                ins = dve.reduce_sum(rsum[:, hs, :], prob[:, hs, :, :], AX.X)
            link(ins)
            dve.reciprocal(rsum[:, :, :], rsum[:, :, :]).then_inc(made["rr"], 1)
            dve.wait_ge(made["rr"], 1)
            dve.wait_ge(dma["wo"], 32)
            hs = slice(0, HEADS // 2)
            dve.tensor_tensor(wos[:, hs, :, :], wo[:, hs, :].unsqueeze(2).to_broadcast([P, HEADS // 2, BH, C]),
                              rsum[:, hs, :].unsqueeze(3).to_broadcast([P, HEADS // 2, BH, C]), ALU.mult).then_inc(made["wos_v"], 1)
            wait_chunk(dve, "z0")
            dve.tensor_copy(z[:, 0, :, :, :], bank("z0")).then_inc(read_v, 1)
            dve.wait_ge(const["m"], 1)
            wait_chunk(dve, "m")
            for l in range(2):
                r = slice(l * C, (l + 1) * C)
                ins = dve.tensor_copy(m[r, :, l, :], bank("m")[r, 0:BH * C].rearrange("p (t j) -> p t j", t=BH))
            ins.then_inc(read_v, 1)
            wait_chunk(dve, "o")
            dve.tensor_tensor(t2[:, :, :], bank("o").rearrange("p (i c) -> p i c", c=C), t[:, :, :], ALU.add).then_inc(read_v, 1)
            wait_read(dve, "o")
            layer_norm(f, t2, made["f"])

            dve.wait_ge(made["fsum"], 2)
            dve.wait_ge(dma["wr"], 48)
            for i in range(BH):
                dve.tensor_scalar(rl[:, i, :, :], wr[:, :, :], fsum[:, i:i + 1], None, ALU.mult).then_inc(made["rl"], 1)
            wait_chunk(dve, "logits")
            L, E = rt[:, 0, :, :], rt[:, 1, :, :]

            def over(v):
                return v.unsqueeze(2).to_broadcast([P, B, EXP])

            dve.tensor_tensor(L, bank("logits")[:, 0:B * EXP].rearrange("p (b e) -> p b e", b=B),
                              br[:, :].unsqueeze(1).to_broadcast([P, B, EXP]), ALU.add).then_inc(read_v, 1)
            wait_read(dve, "logits")
            mx, sm, ld, sc = rs[:, 0, 0:B], rs[:, 1, 0:B], rs[:, 2, :], rs[:, 3, :]
            link(dve.reduce_max(mx, L, AX.X))
            dve.tensor_tensor(L, L, over(mx), ALU.subtract).then_inc(made["logit"], 1)
            dve.wait_ge(made["exp1"], 1)
            link(dve.reduce_sum(sm, E, AX.X))
            link(dve.reciprocal(sm, sm))
            link(dve.tensor_tensor(E, E, over(sm), ALU.mult))
            link(dve.reduce_sum(ld, E.rearrange("p b e -> p e b"), AX.X))
            link(dve.reciprocal(ld, ld))
            link(dve.tensor_scalar(sc, ld, float(CAPACITY) / HW, 1.0, ALU.mult, ALU.min))
            link(dve.tensor_tensor(L, E, sc.unsqueeze(1).to_broadcast([P, B, EXP]), ALU.mult))
            link(dve.reduce_max(mx, L, AX.X))
            dve.tensor_tensor(L, L, over(mx), ALU.subtract).then_inc(made["logit2"], 1)
            dve.wait_ge(made["exp2"], 1)
            link(dve.reduce_sum(sm, E, AX.X))
            link(dve.reciprocal(sm, sm))
            link(dve.tensor_tensor(E, E, over(sm), ALU.mult))
            for b in range(B):
                ins = dve.max(top[:, b, :], E[:, b, :])
            link(ins)
            dve.tensor_tensor(rs[:, 5, 0:B], top[:, :, 1], top[:, :, 0], ALU.subtract).then_inc(made["dtop"], 1)
            for b in range(B):
                ins = dve.max_index(topi[:, b, :], top[:, b, :], E[:, b, :])
            ins.then_inc(made["topi"], 1)
            dve.wait_ge(made["topi"], 1)
            chosen = [[dve.value_load(topi[0:1, b, k:k + 1], min_val=0, max_val=EXP - 1) for k in range(TOPK)] for b in range(B)]
            dve.wait_ge(dma["w_ffn"], 48)
            for b in range(B):
                t_, l = divmod(b, 2)
                r = slice(l * C, (l + 1) * C)
                for k in range(TOPK):
                    ins = dve.tensor_copy(w1s[r, t_, k, :].unsqueeze(1), fw1[r, bass.ds(chosen[b][k], 1), :])
                    ins.then_inc(made["w1s"], 1)
            wait_read(dve, "b1T")
            for b in range(B):
                for k in range(TOPK):
                    ins = dve.tensor_copy(b1s[:, b, k:k + 1], fb1T[:, bass.ds(chosen[b][k], 1)])
            ins.then_inc(made["b1s"], 1)
            dve.wait_ge(made["etop"], 1)
            link(dve.tensor_scalar(gate[:, :, 0], gate[:, :, 1], 1.0, None, ALU.add))
            link(dve.reciprocal(gate[:, :, 0], gate[:, :, 0]))
            link(dve.tensor_tensor(gate[:, :, 1], gate[:, :, 1], gate[:, :, 0], ALU.mult))
            for b in range(B):
                for k in range(TOPK):
                    dve.tensor_scalar(w2s[:, b, k, :].unsqueeze(1), fw2[:, bass.ds(chosen[b][k], 1), :], gate[:, b, k:k + 1], None, ALU.mult).then_inc(made["w2s"], 1)
            dve.wait_ge(dma["fb"], 16 * 6)
            for b in range(B):
                ins = dve.tensor_scalar(b2s[:, b, :].unsqueeze(1), fb2[:, bass.ds(chosen[b][0], 1), :], gate[:, b, 0:1], None, ALU.mult)
            link(ins)
            for b in range(B):
                ins = dve.scalar_tensor_tensor(b2s[:, b, :].unsqueeze(1), fb2[:, bass.ds(chosen[b][1], 1), :], gate[:, b, 1:2], b2s[:, b, :].unsqueeze(1), ALU.mult, ALU.add)
            link(ins)
            for i in range(BH):
                ins = dve.tensor_tensor(fb[:, 4 * i:4 * i + 4, :].rearrange("p (s l) c -> p s (l c)", s=NS), f[:, 4 * i:4 * i + 4, :].rearrange("p (s l) c -> p s (l c)", s=NS),
                                        b2s[:, 2 * i:2 * i + 2, :].rearrange("p l c -> p (l c)").unsqueeze(1).to_broadcast([P, NS, P]), ALU.add)
            link(ins)
            wait_chunk(dve, "ffn")
            dve.tensor_tensor(u[:, :, :], bank("ffn").rearrange("p (i c) -> p i c", c=C), fb[:, :, :], ALU.add).then_inc(read_v, 1)
            wait_read(dve, "ffn")
            layer_norm(n, u, made["n"])
            wait_read(dve, "t2T")
            wait_chunk(dve, "nT")
            for i in range(BH):
                dve.scalar_tensor_tensor(res[:, i, :], bank("nT")[:, i * HW:(i + 1) * HW], gb[:, 0:1], t2T[:, i, :], ALU.mult, ALU.add).then_inc(made["res"], 1)

        @block.tensor
        def _(pe):
            def begin(name):
                j = INDEX[name]
                if j >= NBANK:
                    wait_read(pe, CHUNKS[j - NBANK][0])
                return bank(name)

            def mm(dst, lhsT, rhs, start=True, stop=True):
                return pe.matmul(dst, lhsT, rhs, start=start, stop=stop)

            dst = begin("w1T")
            pe.wait_ge(dma["w1"], 16)
            pe.wait_ge(const["rep"], 1)
            for l in range(2):
                ins = mm(dst[l * C:(l + 1) * C, 0:G * 32], w1[:, :], rep[0:CR, :, :])
            ins.then_inc(written, 1)
            dst = begin("w2T")
            pe.wait_ge(dma["w2"], 32)
            pe.wait_ge(const["ident"], 1)
            for g in range(G):
                ins = mm(dst[32 * g:32 * g + 32, 0:K * K], w2l[:, g, :], ident[0:K * K, 0:K * K])
            ins.then_inc(written, 1)
            dst = begin("bn")
            pe.wait_ge(made["bnab"], 1)
            mm(dst[:, 0:2], rep[0:CR + 1, :, :], bn_ab[:, :]).then_inc(written, 1)
            dst = begin("gn")
            pe.wait_ge(const["pair"], 1)
            pe.wait_ge(made["gmv"], 1)
            mm(dst[:, 0:2 * BH], pair[:, :], gmv[:, :, :]).then_inc(written, 1)
            pe.wait_ge(made["xn"], BH)
            wait_read(pe, "w1T")
            for l in range(2):
                r = slice(l * C, (l + 1) * C)
                mm(begin(f"y{l}"), w1T[r, :], xp[r, :, PAD:PAD + H, :]).then_inc(written, 1)
            for i in range(8):
                dst = begin(f"x{i}")
                for q in range(4):
                    t_, r = divmod(4 * i + q, H)
                    ins = pe.transpose(dst[0:WIN, q * P:(q + 1) * P], xp[:, t_, r:r + K, :], ident[:, :])
                ins.then_inc(written, 1)
            dst = begin("wpT")
            pe.wait_ge(dma["wp"], 16)
            for l in range(2):
                ins = mm(dst[l * C:(l + 1) * C, 0:C], wp[:, :], ident[0:C, 0:C])
            ins.then_inc(written, 1)
            wait_read(pe, "w2T")
            wait_read(pe, "y1")
            pe.wait_ge(made["taps"], len(EDGES))
            for half in range(2):
                dsts = [begin(f"w{G * half + g}") for g in range(G)]
                for q in range(8):
                    w = 8 * half + q
                    for g in range(G):
                        r = slice(32 * g, 32 * g + 32)
                        ins = mm(dsts[g][0:WIN, q * C:(q + 1) * C], taps[r, EDGES.index(w) + 1 if w in EDGES else 0, W - 1 - w:W - 1 - w + WIN], y[r, w, :, :, :])
                        if q == 7:
                            ins.then_inc(written, 1)
            for i in range(8):
                wait_read(pe, f"w{i}")
            for i in range(4):
                t_, s = divmod(i, NS)
                wait_read(pe, f"x{2 * i + 1}")
                dst = begin(f"d{i}")
                for q in range(8):
                    r = 8 * s + q
                    for l in range(2):
                        ins = mm(dst[l * C:(l + 1) * C, q * C:(q + 1) * C], xw[:, t_, r, l * C:(l + 1) * C], wt[:, l, t_, r, :, :])
                ins.then_inc(written, 1)
            pe.wait_ge(const["wpg"], 2)
            for i in range(4):
                t_, s = divmod(i, NS)
                wait_read(pe, f"d{i}")
                dst = begin(f"t{i}")[:, 0:P]
                mm(dst, x[:, t_, s * TOK:(s + 1) * TOK], ident[:, :], True, False)
                for g in range(G):
                    ins = mm(dst, dsb[:, g, t_, 8 * s:8 * s + 8, :], wpg[:, g, :, :], False, g == G - 1)
                ins.then_inc(written, 1)
            dst = begin("wvT")
            pe.wait_ge(dma["wv"], 16)
            for i in range(HEADS // 2):
                ins = pe.transpose(dst[:, i * C:(i + 1) * C], wv[:, i * P:(i + 1) * P], ident[0:C, 0:C])
            ins.then_inc(written, 1)
            dst = begin("b1T")
            pe.wait_ge(dma["fb"], 16 * 6)
            pe.transpose(dst[:, 0:EXP], fb1[:, :], ident[0:EXP, 0:EXP]).then_inc(written, 1)
            dst = begin("gram")
            pe.wait_ge(made["e"], 1)
            for t_ in range(BH):
                for s in range(NS):
                    i = 2 * (NS * t_ + s)
                    ins = mm(dst[:, t_ * P:(t_ + 1) * P], e[:, i:i + 2, :], e[:, i:i + 2, :], s == 0, s == NS - 1)
            ins.then_inc(written, 1)
            dst = begin("eT")
            for i in range(4):
                ins = pe.transpose(dst[:, i * P:(i + 1) * P], e[:, 2 * i:2 * i + 2, :], ident[:, :])
            ins.then_inc(written, 1)
            pe.wait_ge(dma["wk"], 32)
            wait_read(pe, "gram")
            for t_ in range(BH):
                mm(begin(f"gk{t_}"), gram[:, t_, :], wk[:, :]).then_inc(written, 1)
            pe.wait_ge(dma["wq"], 32)
            wait_read(pe, "gk0")
            wait_read(pe, "gk1")
            for i in range(2):
                dst = begin(f"attn{i}")
                for q in range(HEADS // 2):
                    hd = i * HEADS // 2 + q
                    ins = mm(dst[:, q * P:(q + 1) * P], wq[:, hd, :, :], gk[:, :, hd, :])
                ins.then_inc(written, 1)
            dst = begin("astat")
            pe.wait_ge(const["blk"], 2)
            pe.wait_ge(made["a"], 1)
            mm(dst[:, 0:4 * HEADS], blk[:, :], ast[:, :, :, :]).then_inc(written, 1)
            pe.wait_ge(made["wos_v"], 1)
            pe.wait_ge(made["wos_g"], 1)
            for l in range(2):
                r = slice(l * C, (l + 1) * C)
                dst = begin(f"z{l}")
                for hd in range(HEADS):
                    for t_ in range(BH):
                        c0 = (hd // 2 * BH + t_) * C
                        o = slice(hd % 2 * C, hd % 2 * C + C)
                        ins = mm(dst[o, c0:c0 + C], prob[r, hd, t_, :], wos[r, hd, t_, :])
                ins.then_inc(written, 1)
            wait_read(pe, "wvT")
            dst = begin("m")
            for l in range(2):
                wait_read(pe, f"z{l}")
                for i in range(HEADS // 2):
                    ins = mm(dst[l * C:(l + 1) * C, 0:BH * C], wvT[:, i, :], z[:, l, i, :, :], i == 0, i == HEADS // 2 - 1)
            ins.then_inc(written, 1)
            dst = begin("o")
            wait_read(pe, "eT")
            wait_read(pe, "m")
            for i in range(4):
                t_, s = divmod(i, NS)
                ins = mm(dst[:, i * P:(i + 1) * P], eT[:, t_, s * TOK:(s + 1) * TOK], m[:, t_, :, :])
            ins.then_inc(written, 1)
            dst = begin("t2T")
            wait_read(pe, "o")
            for i in range(4):
                ins = pe.transpose(dst[:, i * P:(i + 1) * P], t2[:, 2 * i:2 * i + 2, :], ident[:, :])
            ins.then_inc(written, 1)
            dst = begin("fT")
            pe.wait_ge(made["f"], 1)
            for i in range(4):
                ins = pe.transpose(dst[:, i * P:(i + 1) * P], f[:, 2 * i:2 * i + 2, :], ident[:, :])
            ins.then_inc(written, 1)
            dst = begin("logits")
            pe.wait_ge(const["mean"], 1)
            pe.wait_ge(made["rl"], 2)
            mm(dst[:, 0:B * EXP], mean_t[:, :], rl[:, :, :, :]).then_inc(written, 1)
            for i in range(B * TOPK):
                b, k = divmod(i, TOPK)
                t_, l = divmod(b, 2)
                r = slice(l * C, (l + 1) * C)
                pe.wait_ge(made["w1s"], i + 1)
                mm(begin(f"h{i}")[:, 0:HW], w1s[r, t_, k, :], fT[r, t_, :]).then_inc(written, 1)
            dst = begin("ffn")
            pe.wait_ge(made["w2s"], B * TOPK)
            for b in range(B):
                t_, l = divmod(b, 2)
                wait_read(pe, f"h{TOPK * b + 1}")
                for s in range(NS):
                    c0 = (2 * (NS * t_ + s) + l) * C
                    for k in range(TOPK):
                        ins = mm(dst[:, c0:c0 + C], h[:, b, k, s * TOK:(s + 1) * TOK], w2s[:, b, k, :], k == 0, k == TOPK - 1)
            ins.then_inc(written, 1)
            dst = begin("nT")
            pe.wait_ge(made["n"], 1)
            for i in range(4):
                ins = pe.transpose(dst[:, i * P:(i + 1) * P], n[:, 2 * i:2 * i + 2, :], ident[:, :])
            ins.then_inc(written, 1)


NAMES = ["x", "L0_conv_w1", "L0_conv_gamma", "L0_conv_beta", "L0_conv_mean", "L0_conv_var", "L0_conv_w2", "L0_conv_b2",
         "L0_conv_wp", "L1_attn_Wq", "L1_attn_Wk", "L1_attn_Wv", "L1_attn_Wo", "L1_ffn_Wr", "L1_ffn_br", "L1_ffn_W1",
         "L1_ffn_b1", "L1_ffn_W2", "L1_ffn_b2", "L1_ffn_gamma", "L1_ffn_beta"]


def kernel(**inputs):
    import numpy as np
    import concourse.bacc as bacc
    from concourse.bass_utils import run_bass_kernel_spmd

    nc = bacc.Bacc("TRN2", target_bir_lowering=False, num_devices=1)
    arrays = {"in_" + k: np.ascontiguousarray(inputs[k]) for k in NAMES}
    dram = {k: nc.dram_tensor("in_" + k, arrays["in_" + k].shape, F32, kind="ExternalInput").ap() for k in NAMES}
    out = nc.dram_tensor("out", (B, C, H, W), F32, kind="ExternalOutput").ap()
    build(nc, dram, out)
    r = run_bass_kernel_spmd(nc, [arrays], core_ids=[0])
    return r.results[0]["out"]
```

```python
from contextlib import ExitStack

import concourse.bass as bass
from concourse import mybir

F32 = mybir.dt.float32
BF16 = mybir.dt.bfloat16
I32 = mybir.dt.int32
U32 = mybir.dt.uint32
ALU = mybir.AluOpType
ACT = mybir.ActivationFunctionType
AX = mybir.AxisListType

P = 128
B, C, H, W = 4, 64, 16, 16
HW = H * W
BH = B // 2
TOK = P
NS = HW // TOK
NT = BH * NS * 2
NQ = BH * NS
K = 7
PAD = K // 2
GC = 16
G = C // GC
CR = C // 4
HP = H // 2
WINR = K + 1
TAP0 = 2 * W - 1
TAPS = TAP0 + P + 1
EDGES = [*range(PAD), *range(W - PAD, W)]
PARTS = [(1, 1), (1, 2), (1, 3), (2, 1), (2, 2), (3, 1)]
BIAS0 = CR * len(PARTS)
HEADS = 8
EXP = 8
FF = 128
TOPK = 2
CAPACITY = -(-B * HW * 5 // (4 * EXP))
EPS = 1e-5
BANK = 512
NBANK = 8
C_ID, C_REP, C_PAIR, C_BLK, C_MASK = 0, P, 2 * P, 3 * P, 4 * P
C_GROUP = C_MASK + 4
C_MEAN = C_GROUP + 2 * G
C_END = C_MEAN + 1
WOS_V = 5
WARM = {"start": 8, "gn": 3, "norm": 1, "softmax": 2, "routing": 2}

CHUNKS = [
    ("w1T", "V"), ("gn", "V"), ("w2T", "A"), ("y0", "A"), ("y1", "A"), ("bn", "V"), ("wrep", "V"),
    ("x0", "A"), ("x1", "A"), ("x2", "A"), ("x3", "A"),
    ("wpT", "A"),
    ("w0", "V"), ("w1", "A"), ("w2", "V"), ("w3", "A"), ("w4", "V"), ("w5", "A"), ("w6", "V"), ("w7", "A"),
    ("d0", "V"), ("d1", "A"), ("d2", "V"), ("d3", "A"),
    ("t0", "A"), ("t1", "A"), ("t2", "A"), ("t3", "A"),
    ("wvT", "A"), ("b1T", "A"),
    ("gram", "V"), ("eT", "A"), ("gks", "V"), ("gk0", "V"), ("gk1", "A"), ("attn0", "A"), ("attn1", "A"), ("astat", "V"),
    ("z0", "V"), ("z1", "A"), ("m", "V"), ("o0", "V"), ("o1", "V"), ("o2", "V"), ("o3", "V"),
    ("t2T", "A"), ("fT", "A"), ("fsum", "V"), ("logits", "V"),
    ("h0", "A"), ("h1", "A"), ("h2", "A"), ("h3", "A"), ("h4", "A"), ("h5", "A"),
    ("h6", "A"), ("h7", "A"), ("ffn0", "V"), ("ffn1", "V"), ("ffn2", "V"), ("ffn3", "V"), ("nT0", "V"), ("nT1", "V"),
]
INDEX = {name: j for j, (name, _) in enumerate(CHUNKS)}


def reads_until(j):
    return sum(1 for _, r in CHUNKS[:j + 1] if r == CHUNKS[j][1])


def build(nc, d, out):
    with ExitStack() as ctx:
        def sb(name, shape, dt=F32):
            return ctx.enter_context(nc.sbuf_tensor(name, shape, dt))

        def sem(name):
            return ctx.enter_context(nc.semaphore(name))

        consts = sb("consts", [P, C_END])
        ident = consts[:, C_ID:C_ID + P]
        rep = consts[:, C_REP:C_REP + P]
        pair = consts[:, C_PAIR:C_PAIR + P]
        blk = consts[:, C_BLK:C_BLK + P]
        mask = consts[:, C_MASK:C_MASK + 4]
        gmask = consts[:, C_GROUP:C_GROUP + 2 * G]
        meanw = consts[:, C_MEAN:C_MEAN + 1]
        ones = sb("ones", [P, P])
        eps = sb("eps", [P, 1])
        zeros = sb("zeros", [P, BANK], BF16)
        w1 = sb("w1", [CR, C])
        bnv = sb("bnv", [CR, 4])
        bn_ab = sb("bn_ab", [CR + 1, 2])
        bn_t = sb("bn_t", [CR, 4])
        w2l = sb("w2l", [K * K, G, CR + 1])
        w2T = sb("w2T", [CR + 1, G * K * K])
        w2a = sb("w2a", [P, G * K * K], BF16)
        w2r = sb("w2r", [P, G * K * K])
        w2b = sb("w2b", [P, G * K * K], BF16)
        w2c = sb("w2c", [P, G, K, K], BF16)
        wp = sb("wp", [C, C])
        wpT = sb("wpT", [P, C])
        wpg = sb("wpg", [P, G, 2, C])
        wq = sb("wq", [P, HEADS, 2, C])
        wk = sb("wk", [P, HEADS * C])
        wv = sb("wv", [C, HEADS * C])
        wvT = sb("wvT", [P, HEADS // 2, C])
        wo = sb("wo", [P, HEADS, C])
        wr = sb("wr", [P, 2, EXP])
        br = sb("br", [P, EXP])
        fw1 = sb("fw1", [P, EXP, FF])
        fw2 = sb("fw2", [P, EXP, C])
        fb1 = sb("fb1", [EXP, FF])
        fb1T = sb("fb1T", [P, EXP])
        fb2 = sb("fb2", [P, EXP, C])
        gb = sb("gb", [P, 2])
        x = sb("x", [P, BH, HW])
        xp = sb("xp", [P, BH, H + 2 * PAD, W])
        gst = sb("gst", [P, BH, 6])
        gmv = sb("gmv", [P, BH, 2])
        gd = sb("gd", [P, BH])
        gs = sb("gs", [P, BH, 2])
        gve = sb("gve", [P, BH])
        gn_t = sb("gn_t", [P, BH])
        gr = sb("gr", [P, BH])
        w1T = sb("w1T", [P, P])
        taps = sb("taps", [P, G, 1 + len(EDGES), TAPS], BF16)
        bns = sb("bns", [P, 2])
        yf = sb("yf", [P, W, 2, 2, BH * HP])
        ya = sb("ya", [P, W, 2, 2, BH * HP], BF16)
        yr = sb("yr", [P, W, 2, 2, BH * HP])
        yb = sb("yb", [P, W, 2, 2, BH * HP], BF16)
        yc = sb("yc", [P, W, 2, 2, BH * HP], BF16)
        xw = sb("xw", [P, BH, HP, P])
        wt = sb("wt", [P, 2, BH, HP, 2, G, W])
        dsb = sb("dsb", [P, G, BH, H, W])
        t = sb("t", [P, NT, C])
        e = sb("e", [P, NT, C])
        eT = sb("eT", [P, BH, HW])
        gram = sb("gram", [P, BH, P])
        gk = sb("gk", [P, BH, HEADS, C])
        a = sb("a", [P, HEADS, BH, C])
        ac = sb("ac", [P, HEADS, BH, C])
        asq = sb("asq", [P, HEADS, BH, C])
        amax = sb("amax", [P, HEADS, BH])
        ast = sb("ast", [P, 2, HEADS, BH])
        asc = sb("asc", [P, 2, HEADS, BH])
        wqs = sb("wqs", [P, HEADS])
        wks = sb("wks", [P, HEADS])
        ar = sb("ar", [P, HEADS, BH])
        prob = sb("prob", [P, HEADS, BH, C])
        rsum = sb("rsum", [P, HEADS, BH])
        wos = sb("wos", [P, HEADS, BH, C])
        z = sb("z", [P, 2, HEADS // 2, BH, C])
        m = sb("m", [P, BH, 2, C])
        t2 = sb("t2", [P, NT, C])
        t2T = sb("t2T", [P, BH, HW])
        f = sb("f", [P, NT, C])
        fT = sb("fT", [P, BH, HW])
        fmean = sb("fmean", [P, BH])
        rl = sb("rl", [P, BH, 2, EXP])
        rt = sb("rt", [P, 2, B, EXP])
        rs = sb("rs", [P, 6, EXP])
        top = sb("top", [P, B, 8])
        topi = sb("topi", [P, B, 8], U32)
        pick = sb("pick", [P, B, TOPK], U32)
        gate = sb("gate", [P, B, TOPK])
        w1s = sb("w1s", [P, BH, TOPK, FF])
        w2s = sb("w2s", [P, B, TOPK, C])
        b2s = sb("b2s", [P, B, C])
        h = sb("h", [P, B, TOPK, HW])
        fb = sb("fb", [P, NT, C])
        u = sb("u", [P, NT, C])
        n = sb("n", [P, NT, C])
        res = sb("res", [P, BH, HW])
        norm = {k: (sb(k + "_st", [P, NT, 6]), sb(k + "_mv", [P, NT, 2]), sb(k + "_sd", [P, NT])) for k in "efn"}

        ps = ctx.enter_context(nc.psum_tensor("ps", [P, NBANK, BANK], F32))

        def bank(name):
            return ps[:, INDEX[name] % NBANK, :]

        written = sem("psum_written")
        read_v = sem("psum_read_by_vector")
        read_a = sem("psum_read_by_scalar")
        v_seq = sem("vector_steps")
        dma = {k: sem("loaded_" + k) for k in ("const", "x", "w1", "bn", "w2", "wp", "wq", "wk", "wv", "wo", "wr", "w_ffn", "fb1", "fb2", "gb", "br")}
        stored = sem("stored")
        const = {k: sem("made_" + k) for k in ("wq", "wr", "taps", "gram", "m", "xp", "wpg", "ones", "eps", "zeros")}
        made = {k: sem("sb_" + k) for k in (
            "w2c", "taps", "bns", "bnab", "bn_var", "bn_std", "gmv", "g_var", "g_std", "xn", "yf", "ya", "yc",
            "wks", "wqs", "qk", "c", "cr", "ast", "a_var", "a_std", "asq", "a", "amax", "prob", "rr", "wos_g", "wos_v", "ar",
            "rl", "logit", "exp1", "logit2", "exp2", "dtop", "etop", "pick", "picked", "w1s", "w2s", "b2s", "fb", "res", "gate",
            "e", "f", "n", "e_g", "f_g", "n_g", "e_rs", "f_rs", "n_rs", "e_var", "e_std", "f_var", "f_std", "n_var", "n_std")}
        block = ctx.enter_context(nc.Block())

        def tap_view(g, v, lo, hi):
            at = TAP0 - PAD
            return taps[:, g, v, at:at + K * W].rearrange("p (i j) -> p i j", j=W)[:, :, lo:hi]

        def wait_chunk(eng, name):
            eng.wait_ge(written, INDEX[name] + 1)

        def wait_read(eng, name):
            j = INDEX[name]
            eng.wait_ge(read_v if CHUNKS[j][1] == "V" else read_a, reads_until(j))

        def involution_reads(eng, copy, names, read):
            for name in names:
                wait_chunk(eng, name)
                src = bank(name)
                if name == "wpT":
                    copy(wpT[:, :], src[:, 0:C]).then_inc(read, 1)
                    continue
                i = int(name[1:])
                if name[0] == "x":
                    t_, q = divmod(4 * i, HP)
                    copy(xw[:, t_, q:q + 4, :], src).then_inc(read, 1)
                elif name[0] == "w":
                    g, w0 = i % G, 8 * (i // G)
                    copy(wt[:, :, :, :, :, g, w0:w0 + 8].rearrange("p l t q r w -> p (l t q) r w"),
                         src.rearrange("p (w r q) -> p q r w", w=8, r=2)).then_inc(read, 1)
                else:
                    t_, s = divmod(i, NS)
                    copy(dsb[:, :, t_, 8 * s:8 * s + 8, :].rearrange("p g h w -> p h g w"),
                         src.rearrange("p (h g w) -> p h g w", h=8, g=G)).then_inc(read, 1)

        def edge_taps(copy, v, done):
            w = EDGES[v - 1]
            lo, hi = max(0, PAD - w), min(K, W + PAD - w)
            at = TAP0 - PAD
            dst = taps[:, :, v, at:at + K * W].rearrange("p g (i j) -> p g i j", j=W)[:, :, :, lo:hi]
            copy(dst, w2c[:, :, :, lo:hi]).then_inc(done, 1)

        @block.sync
        def _(sp):
            sp.dma_start(x[:, :, :], d["x"].rearrange("(t u) c h w -> (u c) t (h w)", t=BH)).then_inc(dma["x"], 16)
            sp.dma_start(w2l[:, :, 0:CR], d["L0_conv_w2"].rearrange("(g k) c -> k g c", g=G)).then_inc(dma["w2"], 16)
            sp.dma_start(w2l[:, :, CR:CR + 1], d["L0_conv_b2"].rearrange("(g k o) -> k g o", g=G, o=1), allow_slow_non_contiguous=True).then_inc(dma["w2"], 16)
            for i, name in enumerate(("gamma", "beta", "mean", "var")):
                sp.dma_start(bnv[:, i:i + 1], d["L0_conv_" + name].rearrange("(c o) -> c o", o=1)).then_inc(dma["bn"], 16)
            sp.dma_start(wp[:, :], d["L0_conv_wp"]).then_inc(dma["wp"], 16)
            for l in range(2):
                sp.dma_start(wk[l * C:(l + 1) * C, :], d["L1_attn_Wk"]).then_inc(dma["wk"], 16)
            sp.wait_ge(const["wq"], 1)
            for l in range(2):
                sp.dma_start(wq[l * C:(l + 1) * C, :, l, :], d["L1_attn_Wq"].rearrange("c (h e) -> c h e", h=HEADS)).then_inc(dma["wq"], 16)
            sp.dma_start(wv[:, :], d["L1_attn_Wv"]).then_inc(dma["wv"], 16)
            sp.dma_start(fb1[:, :], d["L1_ffn_b1"]).then_inc(dma["fb1"], 16)
            for l in range(2):
                sp.dma_start(wo[l * C:(l + 1) * C, :, :], d["L1_attn_Wo"].rearrange("(e h) j -> e h j", h=HEADS)).then_inc(dma["wo"], 16)
            for l in range(2):
                sp.dma_start(gb[l * C:(l + 1) * C, 0:1], d["L1_ffn_gamma"].rearrange("(c o) -> c o", o=1)).then_inc(dma["gb"], 16)
                sp.dma_start(gb[l * C:(l + 1) * C, 1:2], d["L1_ffn_beta"].rearrange("(c o) -> c o", o=1)).then_inc(dma["gb"], 16)
            for l in range(2):
                sp.dma_start(fw1[l * C:(l + 1) * C, :, :], d["L1_ffn_W1"].rearrange("e c f -> c e f")).then_inc(dma["w_ffn"], 16)
            sp.dma_start(fw2[:, :, :], d["L1_ffn_W2"].rearrange("e f j -> f e j")).then_inc(dma["w_ffn"], 16)
            for i in range(BH):
                sp.wait_ge(made["res"], i + 1)
                sp.dma_start(out.rearrange("(t u) c h w -> (u c) t (h w)", t=BH)[:, i, :], res[:, i, :]).then_inc(stored, 16)
            sp.wait_ge(stored, 16 * BH)

        @block.gpsimd
        def _(pool):
            def zero(ap, name):
                return pool.memset(ap, 0.0).then_inc(const[name], 1)

            def norm_apply(k, dst, src):
                _, mv, sd = norm[k]
                for i in range(NQ):
                    pool.wait_ge(made[k + "_rs"], i + 1)
                    j = 2 * i + 1
                    pool.tensor_scalar(dst[:, j, :], src[:, j, :], mv[:, j, 0:1], sd[:, j:j + 1], ALU.subtract, ALU.mult).then_inc(made[k + "_g"], 1)

            zero(xp[:, :, 0:PAD, :], "xp")
            zero(xp[:, :, PAD + H:, :], "xp")
            zero(taps[:, 0:G // 2, :, :], "taps")
            zero(wr[:, :, :], "wr")
            zero(wq[:, :, :, :], "wq")
            pool.wait_ge(const["wr"], 1)
            for l in range(2):
                pool.dma_start(wr[l * C:(l + 1) * C, l, :], d["L1_ffn_Wr"]).then_inc(dma["wr"], 16)
            pool.dma_start(br[:, :], d["L1_ffn_br"].rearrange("(o e) -> o e", o=1).broadcast_to([P, EXP])).then_inc(dma["br"], 16)
            pool.dma_start(fb2[:, :, :], d["L1_ffn_b2"].rearrange("(o e) j -> o e j", o=1).broadcast_to([P, EXP, C])).then_inc(dma["fb2"], 16)
            pool.wait_ge(made["w2c"], 1)
            pool.wait_ge(const["taps"], 2)
            for v in (1, 2):
                edge_taps(pool.tensor_copy, v, made["taps"])
            zero(gram[:, :, :], "gram")
            zero(m[:, :, :, :], "m")
            pool.wait_ge(dma["const"], 16)
            wait_read(pool, "wpT")
            pool.tensor_tensor(wpg[:, :, :, :].rearrange("p g l c -> p l g c"), wpT[:, :].unsqueeze(1).unsqueeze(1).to_broadcast([P, 2, G, C]),
                               gmask.rearrange("p (l g) -> p l g", l=2).unsqueeze(3).to_broadcast([P, 2, G, C]), ALU.mult).then_inc(const["wpg"], 1)
            norm_apply("e", e, t)
            hh = slice(HEADS // 2, HEADS)
            pool.wait_ge(made["amax"], 2)
            pool.tensor_tensor(ac[:, hh, :, :], a[:, hh, :, :], amax[:, hh, :].unsqueeze(3).to_broadcast([P, HEADS // 2, BH, C]), ALU.subtract).then_inc(made["c"], 1)
            pool.wait_ge(made["c"], 1)
            pool.wait_ge(made["ar"], 1)
            pool.tensor_tensor(ac[:, hh, :, :], ac[:, hh, :, :], ar[:, hh, :].unsqueeze(3).to_broadcast([P, HEADS // 2, BH, C]), ALU.mult).then_inc(made["cr"], 1)
            pool.wait_ge(made["rr"], 1)
            pool.wait_ge(dma["wo"], 32)
            hh = slice(WOS_V, HEADS)
            pool.tensor_tensor(wos[:, hh, :, :], wo[:, hh, :].unsqueeze(2).to_broadcast([P, HEADS - WOS_V, BH, C]),
                               rsum[:, hh, :].unsqueeze(3).to_broadcast([P, HEADS - WOS_V, BH, C]), ALU.mult).then_inc(made["wos_g"], 1)
            norm_apply("f", f, t2)
            pool.wait_ge(made["f"], NQ)
            pool.wait_ge(made["f_g"], NQ)
            for i in range(BH):
                pool.wait_ge(made["b2s"], i + 1)
                pool.tensor_tensor(fb[:, 4 * i:4 * i + 4, :].rearrange("p (s l) c -> p s (l c)", s=NS), f[:, 4 * i:4 * i + 4, :].rearrange("p (s l) c -> p s (l c)", s=NS),
                                   b2s[:, 2 * i:2 * i + 2, :].rearrange("p l c -> p (l c)").unsqueeze(1).to_broadcast([P, NS, P]), ALU.add).then_inc(made["fb"], 1)
            norm_apply("n", n, u)

        @block.scalar
        def _(act):
            act.dma_start(consts[:, :], d["consts"]).then_inc(dma["const"], 16)
            act.dma_start(w1[:, :], d["L0_conv_w1"]).then_inc(dma["w1"], 16)
            act.preload_act_table(ACT.Sqrt)

            def copy(dst, src):
                return act.activation(dst, src, ACT.Copy)

            def norm_root(k, i):
                act.wait_ge(made[k + "_var"], i + 1)
                act.activation(norm[k][2][:, 2 * i:2 * i + 2], norm[k][1][:, 2 * i:2 * i + 2, 1], ACT.Sqrt, bias=eps[:, :]).then_inc(made[k + "_std"], 1)

            act.wait_ge(const["eps"], 1)
            act.wait_ge(made["g_var"], 1)
            act.activation(gr[:, :], gd[:, :], ACT.Sqrt, bias=eps[:, :]).then_inc(made["g_std"], 1)
            act.wait_ge(dma["bn"], 64)
            act.activation(bn_t[:, 0:1], bnv[:, 3:4], ACT.Sqrt, bias=eps[0:CR, :]).then_inc(made["bn_std"], 1)
            wait_chunk(act, "w2T")
            copy(w2T[:, :], bank("w2T")[0:CR + 1, 0:G * K * K]).then_inc(read_a, 1)
            act.wait_ge(made["bns"], 1)
            for l in range(2):
                wait_chunk(act, f"y{l}")
                src = bank(f"y{l}").rearrange("p (q r w) -> p q r w", r=2, w=W)
                act.activation(yf[:, :, :, l, :].rearrange("p w r q -> p q r w"), src, ACT.Relu,
                               bias=bns[:, 1:2], scale=bns[:, 0:1]).then_inc(made["yf"], 1)
                act.activation(ya[:, :, :, l, :].rearrange("p w r q -> p q r w"), src, ACT.Relu,
                               bias=bns[:, 1:2], scale=bns[:, 0:1]).then_inc(read_a, 1)
            act.wait_ge(made["w2c"], 1)
            act.wait_ge(const["taps"], 2)
            for v in (3, 4):
                edge_taps(copy, v, made["taps"])
            involution_reads(act, copy, [c for c, r in CHUNKS[INDEX["x0"]:INDEX["d3"] + 1] if r == "A"], read_a)

            for i in range(NQ):
                wait_chunk(act, f"t{i}")
                copy(t[:, 2 * i:2 * i + 2, :], bank(f"t{i}")[:, 0:P]).then_inc(read_a, 1)
                if i:
                    norm_root("e", i - 1)
            norm_root("e", NQ - 1)
            wait_chunk(act, "wvT")
            copy(wvT[:, :, :], bank("wvT")[:, 0:HEADS // 2 * C]).then_inc(read_a, 1)
            wait_chunk(act, "b1T")
            copy(fb1T[:, :], bank("b1T")[:, 0:EXP]).then_inc(read_a, 1)
            wait_chunk(act, "eT")
            copy(eT[:, :, :], bank("eT")).then_inc(read_a, 1)
            wait_chunk(act, "gk1")
            copy(gk[:, 1, :, :], bank("gk1")).then_inc(read_a, 1)
            for i in range(2):
                hs = slice(i * HEADS // 2, (i + 1) * HEADS // 2)
                wait_chunk(act, f"attn{i}")
                copy(a[:, hs, :, :], bank(f"attn{i}")).then_inc(read_a, 1)
            for i in range(2):
                hs = slice(i * HEADS // 2, (i + 1) * HEADS // 2)
                act.wait_ge(read_a, reads_until(INDEX[f"attn{i}"]))
                act.activation(asq[:, hs, :, :], a[:, hs, :, :], ACT.Square).then_inc(made["asq"], 1)
            act.wait_ge(made["a_var"], 1)
            act.activation(ar[:, :, :], asc[:, 1, :, :], ACT.Sqrt, bias=eps[:, :]).then_inc(made["a_std"], 1)
            act.preload_act_table(ACT.Exp)
            act.wait_ge(made["ast"], 1)
            hs = slice(0, HEADS // 2)
            act.activation(prob[:, hs, :, :], ac[:, hs, :, :], ACT.Exp).then_inc(made["prob"], 1)
            act.wait_ge(made["cr"], 1)
            hs = slice(HEADS // 2, HEADS)
            act.activation(prob[:, hs, :, :], ac[:, hs, :, :], ACT.Exp).then_inc(made["prob"], 1)
            act.preload_act_table(ACT.Sqrt)
            wait_chunk(act, "z1")
            copy(z[:, 1, :, :, :], bank("z1")).then_inc(read_a, 1)
            for i in range(NQ):
                norm_root("f", i)
            act.preload_act_table(ACT.Exp)
            act.wait_ge(dma["gb"], 64)
            wait_chunk(act, "t2T")
            act.activation(t2T[:, :, :], bank("t2T"), ACT.Identity, bias=gb[:, 1:2]).then_inc(read_a, 1)
            wait_chunk(act, "fT")
            copy(fT[:, :, :], bank("fT")).then_inc(read_a, 1)
            act.wait_ge(made["logit"], 1)
            act.activation(rt[:, 1, :, :], rt[:, 0, :, :], ACT.Exp).then_inc(made["exp1"], 1)
            act.wait_ge(made["logit2"], 1)
            act.activation(rt[:, 1, :, :], rt[:, 0, :, :], ACT.Exp).then_inc(made["exp2"], 1)
            act.wait_ge(made["dtop"], 1)
            act.activation(gate[:, :, 1:2], rs[:, 4, 0:B].unsqueeze(2), ACT.Exp).then_inc(made["etop"], 1)
            act.preload_act_table(ACT.Gelu)
            act.wait_ge(made["pick"], 1)
            _, chosen = nc.values_load_multi_w_load_instructions(
                pick[0:1, :, :].rearrange("p b k -> p (b k)"), engines=[act.engine], min_val=0, max_val=EXP - 1,
                skip_runtime_bounds_check_because="pick keeps the low three bits only, so it is below EXP")
            act.wait_ge(read_a, reads_until(INDEX["b1T"]))
            for i in range(B * TOPK):
                b, k = divmod(i, TOPK)
                wait_chunk(act, f"h{i}")
                act.activation(h[:, b, k, :], bank(f"h{i}")[:, 0:HW], ACT.Gelu, bias=fb1T[:, bass.ds(chosen[i], 1)]).then_inc(read_a, 1)
            act.preload_act_table(ACT.Sqrt)
            for i in range(NQ):
                norm_root("n", i)

        @block.vector
        def _(dve):
            steps = [0]

            def link(ins):
                steps[0] += 1
                ins.then_inc(v_seq, 1)
                dve.wait_ge(v_seq, steps[0])

            def newton(r, v, tmp):
                link(dve.tensor_tensor(tmp, r, r, ALU.mult))
                link(dve.scalar_tensor_tensor(tmp, tmp, -0.5, v, ALU.mult, ALU.mult))
                link(dve.scalar_tensor_tensor(r, tmp, 1.5, r, ALU.add, ALU.mult))

            def norm_stats(k, src, i):
                st, mv, _ = norm[k]
                for j in (2 * i, 2 * i + 1):
                    ins = dve.bn_stats(st[:, j, :], src[:, j, :])
                link(ins)
                dve.bn_aggr(mv[:, 2 * i, :], st[:, 2 * i, :])
                dve.bn_aggr(mv[:, 2 * i + 1, :], st[:, 2 * i + 1, :]).then_inc(made[k + "_var"], 1)

            def norm_apply(k, dst, src, i):
                _, mv, sd = norm[k]
                dve.wait_ge(made[k + "_var"], i + 1)
                dve.wait_ge(made[k + "_std"], i + 1)
                dve.reciprocal(sd[:, 2 * i:2 * i + 2], sd[:, 2 * i:2 * i + 2]).then_inc(made[k + "_rs"], 1)
                dve.wait_ge(made[k + "_rs"], i + 1)
                j = 2 * i
                dve.tensor_scalar(dst[:, j, :], src[:, j, :], mv[:, j, 0:1], sd[:, j:j + 1], ALU.subtract, ALU.mult).then_inc(made[k], 1)

            dve.memset(eps[:, :], EPS).then_inc(const["eps"], 1)
            dve.memset(zeros[:, :], 0.0).then_inc(const["zeros"], 1)
            dve.memset(ones[:, :], 1.0).then_inc(const["ones"], 1)
            dve.memset(bn_ab[:, 0:1], 0.0)
            link(dve.memset(bn_ab[:, 1:2], 1.0))
            dve.memset(taps[:, G // 2:, :, :], 0.0).then_inc(const["taps"], 1)
            dve.wait_ge(dma["x"], 16)
            for i in range(BH):
                ins = dve.bn_stats(gst[:, i, :], x[:, i, :])
            link(ins)
            for i in range(BH):
                ins = dve.bn_aggr(gmv[:, i, :], gst[:, i, :])
            ins.then_inc(made["gmv"], 1)
            wait_chunk(dve, "w1T")
            dve.tensor_copy(w1T[:, :], bank("w1T")[:, 0:P]).then_inc(read_v, 1)
            dve.wait_ge(made["gmv"], 1)
            wait_chunk(dve, "gn")
            dve.tensor_copy(gs[:, :, :], bank("gn")[:, 0:2 * BH]).then_inc(read_v, 1)
            dve.wait_ge(read_v, reads_until(INDEX["gn"]))
            link(dve.tensor_tensor(gd[:, :], gmv[:, :, 0], gs[:, :, 0], ALU.subtract))
            link(dve.tensor_tensor(gd[:, :], gd[:, :], gd[:, :], ALU.mult))
            dve.tensor_tensor(gd[:, :], gd[:, :], gs[:, :, 1], ALU.add).then_inc(made["g_var"], 1)
            dve.wait_ge(made["g_var"], 1)
            dve.tensor_scalar(gve[:, :], gd[:, :], EPS, None, ALU.add)
            dve.wait_ge(made["g_std"], 1)
            link(dve.reciprocal(gr[:, :], gr[:, :]))
            newton(gr[:, :], gve[:, :], gn_t[:, :])
            for i in range(BH):
                dve.tensor_scalar(xp[:, i, PAD:PAD + H, :], x[:, i, :].rearrange("p (h w) -> p h w", h=H),
                                  gs[:, i, 0:1], gr[:, i:i + 1], ALU.subtract, ALU.mult).then_inc(made["xn"], 1)
            dve.wait_ge(made["bn_std"], 1)
            dve.wait_ge(dma["bn"], 64)
            dve.tensor_scalar(bn_t[:, 3:4], bnv[:, 3:4], EPS, None, ALU.add)
            link(dve.reciprocal(bn_t[:, 1:2], bn_t[:, 0:1]))
            newton(bn_t[:, 1:2], bn_t[:, 3:4], bn_t[:, 2:3])
            link(dve.tensor_tensor(bn_ab[0:CR, 0:1], bnv[:, 0:1], bn_t[:, 1:2], ALU.mult))
            link(dve.tensor_tensor(bn_t[:, 2:3], bnv[:, 2:3], bn_ab[0:CR, 0:1], ALU.mult))
            dve.tensor_tensor(bn_ab[0:CR, 1:2], bnv[:, 1:2], bn_t[:, 2:3], ALU.subtract).then_inc(made["bnab"], 1)
            wait_chunk(dve, "bn")
            dve.tensor_copy(bns[:, :], bank("bn")[:, 0:2]).then_inc(made["bns"], 1)
            dve.wait_ge(made["bns"], 1)
            dve.sem_inc(read_v, 1)
            dve.wait_ge(dma["const"], 16)
            wait_chunk(dve, "wrep")
            src = bank("wrep")[:, 0:G * K * K]
            link(dve.tensor_copy(w2a[:, :], src))
            dve.scalar_tensor_tensor(w2r[:, :], w2a[:, :], mask[:, 2:3], src, ALU.mult, ALU.add).then_inc(read_v, 1)
            dve.wait_ge(read_v, reads_until(INDEX["wrep"]))
            link(dve.tensor_copy(w2b[:, :], w2r[:, :]))
            dve.scalar_tensor_tensor(w2c[:, :, :, :].rearrange("p g i j -> p (g i j)"), w2b[:, :], mask[:, 3:4], w2r[:, :], ALU.mult, ALU.add).then_inc(made["w2c"], 1)
            dve.wait_ge(made["w2c"], 1)
            dve.wait_ge(const["taps"], 2)
            at = TAP0 - PAD
            dve.tensor_copy(taps[:, :, 0, at:at + K * W].rearrange("p g (i j) -> p g i j", j=W)[:, :, :, 0:K], w2c[:, :, :, :]).then_inc(made["taps"], 1)
            for v in (5, 6):
                edge_taps(dve.tensor_copy, v, made["taps"])

            def split_y(half):
                ws = slice(8 * half, 8 * half + 8)
                dve.wait_ge(made["yf"], 2)
                wait_read(dve, "y1")
                def flat(v):
                    return v[:, ws, :, :, :].rearrange("p w r l q -> p (w r l q)")
                link(dve.scalar_tensor_tensor(flat(yr), flat(ya), mask[:, 0:1], flat(yf), ALU.mult, ALU.add))
                link(dve.tensor_copy(flat(yb), flat(yr)))
                dve.scalar_tensor_tensor(flat(yc), flat(yb), mask[:, 1:2], flat(yr), ALU.mult, ALU.add).then_inc(made["yc"], 1)

            mine = [c for c, r in CHUNKS[INDEX["x0"]:INDEX["d3"] + 1] if r == "V"]
            split_y(0)
            split_y(1)
            involution_reads(dve, dve.tensor_copy, mine, read_v)
            dve.wait_ge(dma["wq"], 32)
            dve.wait_ge(dma["wk"], 32)
            dve.reduce_sum(wks[:, :], wk[:, :].rearrange("p (h e) -> p h e", h=HEADS), AX.X).then_inc(made["wks"], 1)
            for l in range(2):
                r = slice(l * C, (l + 1) * C)
                dve.reduce_sum(wqs[r, :], wq[r, :, l, :], AX.X).then_inc(made["wqs"], 1)

            for i in range(NQ):
                wait_read(dve, f"t{i}")
                norm_stats("e", t, i)
                if i:
                    norm_apply("e", e, t, i - 1)
            norm_apply("e", e, t, NQ - 1)
            dve.wait_ge(const["gram"], 1)
            wait_chunk(dve, "gram")
            gr_ps = bank("gram")[:, 0:BH * P].rearrange("p (t q) -> p t q", t=BH)
            for l in range(2):
                r = slice(l * C, (l + 1) * C)
                ins = dve.tensor_copy(gram[r, :, r], gr_ps[r, :, r])
            ins.then_inc(read_v, 1)
            dve.wait_ge(made["wqs"], 2)
            wait_chunk(dve, "gks")
            dve.tensor_tensor(ast[:, 0, :, :], bank("gks")[:, 0:BH * HEADS].rearrange("p (t h) -> p h t", t=BH),
                              wqs[:, :].unsqueeze(2).to_broadcast([P, HEADS, BH]), ALU.mult).then_inc(read_v, 1)
            wait_chunk(dve, "gk0")
            dve.tensor_copy(gk[:, 0, :, :], bank("gk0")).then_inc(read_v, 1)
            for i in range(2):
                hs = slice(i * HEADS // 2, (i + 1) * HEADS // 2)
                wait_read(dve, f"attn{i}")
                dve.reduce_max(amax[:, hs, :], a[:, hs, :, :], AX.X).then_inc(made["amax"], 1)
            for i in range(2):
                hs = slice(i * HEADS // 2, (i + 1) * HEADS // 2)
                dve.wait_ge(made["asq"], i + 1)
                ins = dve.reduce_sum(ast[:, 1, hs, :], asq[:, hs, :, :], AX.X)
            ins.then_inc(made["a"], 1)
            hs = slice(0, HEADS // 2)
            dve.wait_ge(made["amax"], 1)
            link(dve.tensor_tensor(ac[:, hs, :, :], a[:, hs, :, :], amax[:, hs, :].unsqueeze(3).to_broadcast([P, HEADS // 2, BH, C]), ALU.subtract))
            wait_chunk(dve, "astat")
            dve.tensor_copy(asc[:, :, :, :], bank("astat")[:, 0:4 * HEADS]).then_inc(read_v, 1)
            dve.wait_ge(read_v, reads_until(INDEX["astat"]))
            mu, v = asc[:, 0, :, :].rearrange("p h t -> p (h t)"), asc[:, 1, :, :].rearrange("p h t -> p (h t)")
            link(dve.tensor_tensor(mu, mu, mu, ALU.mult))
            dve.tensor_tensor(v, v, mu, ALU.subtract).then_inc(made["a_var"], 1)
            dve.wait_ge(made["a_std"], 1)
            dve.reciprocal(ar[:, :, :], ar[:, :, :]).then_inc(made["ar"], 1)
            dve.wait_ge(made["ar"], 1)
            dve.tensor_tensor(ac[:, hs, :, :], ac[:, hs, :, :], ar[:, hs, :].unsqueeze(3).to_broadcast([P, HEADS // 2, BH, C]), ALU.mult).then_inc(made["ast"], 1)
            for i in range(2):
                hs = slice(i * HEADS // 2, (i + 1) * HEADS // 2)
                dve.wait_ge(made["prob"], i + 1)
                ins = dve.reduce_sum(rsum[:, hs, :], prob[:, hs, :, :], AX.X)
            link(ins)
            dve.reciprocal(rsum[:, :, :], rsum[:, :, :]).then_inc(made["rr"], 1)
            dve.wait_ge(made["rr"], 1)
            dve.wait_ge(dma["wo"], 32)
            hs = slice(0, WOS_V)
            dve.tensor_tensor(wos[:, hs, :, :], wo[:, hs, :].unsqueeze(2).to_broadcast([P, WOS_V, BH, C]),
                              rsum[:, hs, :].unsqueeze(3).to_broadcast([P, WOS_V, BH, C]), ALU.mult).then_inc(made["wos_v"], 1)
            wait_chunk(dve, "z0")
            dve.tensor_copy(z[:, 0, :, :, :], bank("z0")).then_inc(read_v, 1)
            dve.wait_ge(const["m"], 1)
            wait_chunk(dve, "m")
            for l in range(2):
                r = slice(l * C, (l + 1) * C)
                ins = dve.tensor_copy(m[r, :, l, :], bank("m")[r, 0:BH * C].rearrange("p (t j) -> p t j", t=BH))
            ins.then_inc(read_v, 1)
            for i in range(NQ):
                wait_chunk(dve, f"o{i}")
                dve.tensor_tensor(t2[:, 2 * i:2 * i + 2, :].rearrange("p i c -> p (i c)"), bank(f"o{i}")[:, 0:P],
                                  t[:, 2 * i:2 * i + 2, :].rearrange("p i c -> p (i c)"), ALU.add).then_inc(read_v, 1)
                wait_read(dve, f"o{i}")
                norm_stats("f", t2, i)
                if i:
                    norm_apply("f", f, t2, i - 1)
            norm_apply("f", f, t2, NQ - 1)

            wait_chunk(dve, "fsum")
            dve.tensor_copy(fmean[:, :], bank("fsum")[:, 0:BH]).then_inc(read_v, 1)
            wait_read(dve, "fsum")
            dve.wait_ge(dma["wr"], 32)
            for i in range(BH):
                dve.tensor_scalar(rl[:, i, :, :], wr[:, :, :], fmean[:, i:i + 1], None, ALU.mult).then_inc(made["rl"], 1)
            dve.wait_ge(dma["br"], 16)
            wait_chunk(dve, "logits")
            L, E = rt[:, 0, :, :], rt[:, 1, :, :]

            def over(v):
                return v.unsqueeze(2).to_broadcast([P, B, EXP])

            dve.tensor_tensor(L, bank("logits")[:, 0:B * EXP].rearrange("p (b e) -> p b e", b=B),
                              br[:, :].unsqueeze(1).to_broadcast([P, B, EXP]), ALU.add).then_inc(read_v, 1)
            wait_read(dve, "logits")
            mx, sm, ld, sc = rs[:, 0, 0:B], rs[:, 1, 0:B], rs[:, 2, :], rs[:, 3, :]
            link(dve.reduce_max(mx, L, AX.X))
            dve.tensor_tensor(L, L, over(mx), ALU.subtract).then_inc(made["logit"], 1)
            dve.wait_ge(made["exp1"], 1)
            link(dve.reduce_sum(sm, E, AX.X))
            link(dve.reciprocal(sm, sm))
            link(dve.tensor_tensor(E, E, over(sm), ALU.mult))
            link(dve.reduce_sum(ld, E.rearrange("p b e -> p e b"), AX.X))
            link(dve.reciprocal(ld, ld))
            link(dve.tensor_scalar(sc, ld, float(CAPACITY) / HW, 1.0, ALU.mult, ALU.min))
            dve.tensor_tensor(L, E, sc.unsqueeze(1).to_broadcast([P, B, EXP]), ALU.mult).then_inc(made["logit2"], 1)
            dve.wait_ge(made["exp2"], 1)
            dve.reduce_sum(sm, E, AX.X)
            for b in range(B):
                ins = dve.max(top[:, b, :], E[:, b, :])
            link(ins)
            dve.reciprocal(sm, sm)
            dve.tensor_tensor(rs[:, 5, 0:B], top[:, :, 1], top[:, :, 0], ALU.subtract)
            for b in range(B):
                ins = dve.max_index(topi[:, b, :], top[:, b, :], E[:, b, :])
            link(ins)
            dve.tensor_tensor(rs[:, 4, 0:B], rs[:, 5, 0:B], sm, ALU.mult).then_inc(made["dtop"], 1)
            dve.tensor_scalar(pick[:, :, :], topi[:, :, 0:TOPK], EXP - 1, None, ALU.bitwise_and).then_inc(made["pick"], 1)
            dve.wait_ge(made["pick"], 1)
            _, chosen = nc.values_load_multi_w_load_instructions(
                pick[0:1, :, :].rearrange("p b k -> p (b k)"), engines=[dve.engine], min_val=0, max_val=EXP - 1,
                skip_runtime_bounds_check_because="pick keeps the low three bits only, so it is below EXP")
            chosen = [[chosen[TOPK * b + k] for k in range(TOPK)] for b in range(B)]
            dve.wait_ge(dma["w_ffn"], 48)
            for b in range(B):
                t_, l = divmod(b, 2)
                r = slice(l * C, (l + 1) * C)
                for k in range(TOPK):
                    dve.tensor_copy(w1s[r, t_, k, :].unsqueeze(1), fw1[r, bass.ds(chosen[b][k], 1), :]).then_inc(made["w1s"], 1)
            dve.wait_ge(made["etop"], 1)
            link(dve.tensor_scalar(gate[:, :, 0], gate[:, :, 1], 1.0, None, ALU.add))
            link(dve.reciprocal(gate[:, :, 0], gate[:, :, 0]))
            dve.tensor_tensor(gate[:, :, 1], gate[:, :, 1], gate[:, :, 0], ALU.mult).then_inc(made["gate"], 1)
            dve.wait_ge(made["gate"], 1)
            for b in range(B):
                for k in range(TOPK):
                    dve.tensor_scalar(w2s[:, b, k, :].unsqueeze(1), fw2[:, bass.ds(chosen[b][k], 1), :], gate[:, b, k:k + 1], None, ALU.mult).then_inc(made["w2s"], 1)
            dve.wait_ge(dma["fb2"], 16)
            for i in range(BH):
                for b in (2 * i, 2 * i + 1):
                    ins = dve.tensor_scalar(b2s[:, b, :].unsqueeze(1), fb2[:, bass.ds(chosen[b][0], 1), :], gate[:, b, 0:1], None, ALU.mult)
                link(ins)
                for b in (2 * i, 2 * i + 1):
                    ins = dve.scalar_tensor_tensor(b2s[:, b, :].unsqueeze(1), fb2[:, bass.ds(chosen[b][1], 1), :], gate[:, b, 1:2], b2s[:, b, :].unsqueeze(1), ALU.mult, ALU.add)
                ins.then_inc(made["b2s"], 1)
            for i in range(NQ):
                dve.wait_ge(made["fb"], i // NS + 1)
                wait_chunk(dve, f"ffn{i}")
                dve.tensor_tensor(u[:, 2 * i:2 * i + 2, :].rearrange("p i c -> p (i c)"), bank(f"ffn{i}")[:, 0:P],
                                  fb[:, 2 * i:2 * i + 2, :].rearrange("p i c -> p (i c)"), ALU.add).then_inc(read_v, 1)
                wait_read(dve, f"ffn{i}")
                norm_stats("n", u, i)
                if i:
                    norm_apply("n", n, u, i - 1)
            norm_apply("n", n, u, NQ - 1)
            wait_read(dve, "t2T")
            dve.wait_ge(dma["gb"], 64)
            for i in range(BH):
                wait_chunk(dve, f"nT{i}")
                dve.scalar_tensor_tensor(res[:, i, :], bank(f"nT{i}")[:, 0:HW], gb[:, 0:1], t2T[:, i, :], ALU.mult, ALU.add).then_inc(made["res"], 1)

        @block.tensor
        def _(pe):
            def begin(name):
                j = INDEX[name]
                if j >= NBANK:
                    wait_read(pe, CHUNKS[j - NBANK][0])
                return bank(name)

            def mm(dst, lhsT, rhs, start=True, stop=True):
                return pe.matmul(dst, lhsT, rhs, start=start, stop=stop)

            def keep_warm(name, n):
                dst = begin(name)
                for _ in range(n):
                    mm(dst, zeros[:, 0:P], zeros[:, :])

            pe.wait_ge(const["zeros"], 1)
            keep_warm("w1T", WARM["start"])
            dst = begin("w1T")
            pe.wait_ge(dma["w1"], 16)
            pe.wait_ge(dma["const"], 16)
            for l in range(2):
                ins = mm(dst[l * C:(l + 1) * C, 0:P], w1[:, :], rep[0:CR, :])
            ins.then_inc(written, 1)
            dst = begin("gn")
            pe.wait_ge(made["gmv"], 1)
            mm(dst[:, 0:2 * BH], pair, gmv[:, :, :]).then_inc(written, 1)
            dst = begin("w2T")
            pe.wait_ge(dma["w2"], 32)
            for g in range(G):
                ins = mm(dst[0:CR + 1, g * K * K:(g + 1) * K * K], w2l[:, g, :], ident[0:K * K, 0:K * K])
            ins.then_inc(written, 1)
            keep_warm("y0", WARM["gn"])
            pe.wait_ge(made["xn"], BH)
            wait_read(pe, "w1T")
            for l in range(2):
                r = slice(l * C, (l + 1) * C)
                mm(begin(f"y{l}"), w1T[r, :], xp[r, :, PAD:PAD + H, :]).then_inc(written, 1)
            dst = begin("bn")
            pe.wait_ge(made["bnab"], 1)
            mm(dst[:, 0:2], rep[0:CR + 1, :], bn_ab[:, :]).then_inc(written, 1)
            dst = begin("wrep")
            wait_read(pe, "w2T")
            mm(dst[:, 0:G * K * K], rep[0:CR + 1, :], w2T[:, :]).then_inc(written, 1)
            pe.wait_ge(const["xp"], 2)
            for i in range(4):
                dst = begin(f"x{i}")
                for j in range(4):
                    t_, q = divmod(4 * i + j, HP)
                    ins = pe.transpose(dst[:, j * P:(j + 1) * P], xp[:, t_, 2 * q:2 * q + WINR, :], ident)
                ins.then_inc(written, 1)
            dst = begin("wpT")
            pe.wait_ge(dma["wp"], 16)
            for l in range(2):
                ins = mm(dst[l * C:(l + 1) * C, 0:C], wp[:, :], ident[0:C, 0:C])
            ins.then_inc(written, 1)
            pe.wait_ge(made["taps"], 1 + len(EDGES))
            for half in range(2):
                pe.wait_ge(made["yc"], half + 1)
                dsts = [begin(f"w{G * half + g}") for g in range(G)]
                for g in range(G):
                    for w in range(8 * half, 8 * half + 8):
                        v = EDGES.index(w) + 1 if w in EDGES else 0
                        for r in range(2):
                            at = TAP0 - W * r - w
                            c0 = ((w - 8 * half) * 2 + r) * 2 * BH * HP
                            ins = mm(dsts[g][:, c0:c0 + 2 * BH * HP], taps[:, g, v, at:at + P], yc[:, w, r, :, :])
                    ins.then_inc(written, 1)
            for i in range(8):
                wait_read(pe, f"w{i}")
            for i in range(4):
                t_, s = divmod(i, NS)
                wait_read(pe, f"x{i}")
                dst = begin(f"d{i}")
                for j in range(4):
                    q = 4 * s + j
                    for l in range(2):
                        ins = mm(dst[l * C:(l + 1) * C, j * P:(j + 1) * P], xw[:, t_, q, l * C:(l + 1) * C], wt[:, l, t_, q, :, :, :])
                ins.then_inc(written, 1)
            pe.wait_ge(const["wpg"], 1)
            for i in range(4):
                t_, s = divmod(i, NS)
                wait_read(pe, f"d{i}")
                dst = begin(f"t{i}")[:, 0:P]
                mm(dst, x[:, t_, s * TOK:(s + 1) * TOK], ident, True, False)
                for g in range(G):
                    ins = mm(dst, dsb[:, g, t_, 8 * s:8 * s + 8, :], wpg[:, g, :, :], False, g == G - 1)
                ins.then_inc(written, 1)
            dst = begin("wvT")
            pe.wait_ge(dma["wv"], 16)
            for i in range(HEADS // 2):
                ins = pe.transpose(dst[:, i * C:(i + 1) * C], wv[:, i * P:(i + 1) * P], ident[0:C, 0:C])
            ins.then_inc(written, 1)
            dst = begin("b1T")
            pe.wait_ge(dma["fb1"], 16)
            pe.transpose(dst[:, 0:EXP], fb1[:, :], ident[0:EXP, 0:EXP]).then_inc(written, 1)
            gram_, eT_ = begin("gram"), begin("eT")
            for i in range(NQ):
                t_, s = divmod(i, NS)
                pe.wait_ge(made["e"], i + 1)
                pe.wait_ge(made["e_g"], i + 1)
                last = mm(gram_[:, t_ * P:(t_ + 1) * P], e[:, 2 * i:2 * i + 2, :], e[:, 2 * i:2 * i + 2, :], s == 0, s == NS - 1)
                if i == NQ - 1:
                    last.then_inc(written, 1)
                ins = pe.transpose(eT_[:, i * P:(i + 1) * P], e[:, 2 * i:2 * i + 2, :], ident)
                if i == NQ - 1:
                    ins.then_inc(written, 1)
                keep_warm("gks", WARM["norm"])
            pe.wait_ge(dma["wk"], 32)
            wait_read(pe, "gram")
            dst = begin("gks")
            pe.wait_ge(made["wks"], 1)
            for t_ in range(BH):
                ins = mm(dst[:, t_ * HEADS:(t_ + 1) * HEADS], gram[:, t_, :], wks[:, :])
            ins.then_inc(written, 1)
            for t_ in range(BH):
                mm(begin(f"gk{t_}"), gram[:, t_, :], wk[:, :]).then_inc(written, 1)
            pe.wait_ge(dma["wq"], 32)
            wait_read(pe, "gk0")
            wait_read(pe, "gk1")
            for i in range(2):
                dst = begin(f"attn{i}")
                for q in range(HEADS // 2):
                    hd = i * HEADS // 2 + q
                    ins = mm(dst[:, q * P:(q + 1) * P], wq[:, hd, :, :], gk[:, :, hd, :])
                ins.then_inc(written, 1)
            for i in range(2):
                pe.wait_ge(made["asq"], i + 1)
                keep_warm("astat", WARM["softmax"])
            dst = begin("astat")
            pe.wait_ge(made["a"], 1)
            mm(dst[:, 0:4 * HEADS], blk, ast[:, :, :, :]).then_inc(written, 1)
            for name, count in (("ar", 1), ("prob", 1), ("prob", 2), ("rr", 1)):
                pe.wait_ge(made[name], count)
                keep_warm("z0", WARM["softmax"])
            dsts = [begin(f"z{l}") for l in range(2)]
            pe.wait_ge(made["wos_v"], 1)
            for hd in range(HEADS):
                if hd == WOS_V:
                    pe.wait_ge(made["wos_g"], 1)
                for l in range(2):
                    r = slice(l * C, (l + 1) * C)
                    for t_ in range(BH):
                        c0 = (hd // 2 * BH + t_) * C
                        o = slice(hd % 2 * C, hd % 2 * C + C)
                        ins = mm(dsts[l][o, c0:c0 + C], prob[r, hd, t_, :], wos[r, hd, t_, :])
                    if hd == HEADS - 1:
                        ins.then_inc(written, 1)
            wait_read(pe, "wvT")
            dst = begin("m")
            for l in range(2):
                wait_read(pe, f"z{l}")
                for i in range(HEADS // 2):
                    ins = mm(dst[l * C:(l + 1) * C, 0:BH * C], wvT[:, i, :], z[:, l, i, :, :], i == 0, i == HEADS // 2 - 1)
            ins.then_inc(written, 1)
            wait_read(pe, "eT")
            wait_read(pe, "m")
            for i in range(NQ):
                t_, s = divmod(i, NS)
                mm(begin(f"o{i}")[:, 0:P], eT[:, t_, s * TOK:(s + 1) * TOK], m[:, t_, :, :]).then_inc(written, 1)
            dst = begin("t2T")
            for i in range(NQ):
                wait_read(pe, f"o{i}")
                ins = pe.transpose(dst[:, i * P:(i + 1) * P], t2[:, 2 * i:2 * i + 2, :], ident)
            ins.then_inc(written, 1)
            fT_, fsum_ = begin("fT"), begin("fsum")
            for i in range(NQ):
                t_, s = divmod(i, NS)
                pe.wait_ge(made["f"], i + 1)
                pe.wait_ge(made["f_g"], i + 1)
                last = pe.transpose(fT_[:, i * P:(i + 1) * P], f[:, 2 * i:2 * i + 2, :], ident)
                if i == NQ - 1:
                    last.then_inc(written, 1)
                ins = mm(fsum_[:, t_:t_ + 1], f[:, 2 * i:2 * i + 2, :], meanw, s == 0, s == NS - 1)
            ins.then_inc(written, 1)
            dst = begin("logits")
            pe.wait_ge(const["ones"], 1)
            pe.wait_ge(made["rl"], BH)
            mm(dst[:, 0:B * EXP], ones[:, :], rl[:, :, :, :]).then_inc(written, 1)
            for name in ("logit", "exp1", "logit2", "exp2", "pick"):
                pe.wait_ge(made[name], 1)
                keep_warm("h0", WARM["routing"])

            def first_layer(i):
                b, k = divmod(i, TOPK)
                t_, l = divmod(b, 2)
                r = slice(l * C, (l + 1) * C)
                pe.wait_ge(made["w1s"], i + 1)
                mm(begin(f"h{i}")[:, 0:HW], w1s[r, t_, k, :], fT[r, t_, :]).then_inc(written, 1)

            def second_layer(i):
                t_, s = divmod(i, NS)
                dst = begin(f"ffn{i}")
                for l in range(2):
                    b = 2 * t_ + l
                    wait_read(pe, f"h{TOPK * b + 1}")
                    pe.wait_ge(made["w2s"], TOPK * (b + 1))
                    for k in range(TOPK):
                        ins = mm(dst[:, l * C:(l + 1) * C], h[:, b, k, s * TOK:(s + 1) * TOK], w2s[:, b, k, :], k == 0, k == TOPK - 1)
                ins.then_inc(written, 1)

            wait_read(pe, "fT")
            for name, _ in CHUNKS[INDEX["h0"]:INDEX["nT0"]]:
                if name[0] == "h":
                    first_layer(int(name[1:]))
                else:
                    second_layer(int(name[3:]))
            for i in range(BH):
                dst = begin(f"nT{i}")
                for s in range(NS):
                    j = NS * i + s
                    pe.wait_ge(made["n"], j + 1)
                    pe.wait_ge(made["n_g"], j + 1)
                    ins = pe.transpose(dst[:, s * P:(s + 1) * P], n[:, 2 * j:2 * j + 2, :], ident)
                ins.then_inc(written, 1)


NAMES = ["x", "L0_conv_w1", "L0_conv_gamma", "L0_conv_beta", "L0_conv_mean", "L0_conv_var", "L0_conv_w2", "L0_conv_b2",
         "L0_conv_wp", "L1_attn_Wq", "L1_attn_Wk", "L1_attn_Wv", "L1_attn_Wo", "L1_ffn_Wr", "L1_ffn_br", "L1_ffn_W1",
         "L1_ffn_b1", "L1_ffn_W2", "L1_ffn_b2", "L1_ffn_gamma", "L1_ffn_beta"]


def shape_constants(np):
    c = np.zeros((P, C_END), np.float32)
    p = np.arange(P)
    c[:, C_ID:C_ID + P] = np.eye(P)
    for i in range(len(PARTS)):
        c[0:CR, C_REP + CR * i:C_REP + CR * (i + 1)] = np.eye(CR)
    c[CR, C_REP + BIAS0:C_REP + BIAS0 + 3] = 1.0
    c[:, C_PAIR:C_PAIR + P] = (p[:, None] // 2 == p[None, :] // 2) * 0.5
    c[:, C_BLK:C_BLK + P] = (p[:, None] // C == p[None, :] // C) / (C * C)
    parts = [q for q in PARTS for _ in range(CR)] + [(1, 1), (1, 2), (1, 3)]
    for row, (yp, wp_) in enumerate(parts):
        c[row, C_MASK:C_MASK + 4] = [-(yp > 1), -(yp > 2), -(wp_ > 1), -(wp_ > 2)]
    c[:, C_GROUP:C_GROUP + 2 * G] = p[:, None] // GC == np.arange(2 * G)[None, :]
    c[:, C_MEAN] = 1.0 / HW
    return c


def kernel(**inputs):
    import numpy as np
    import concourse.bacc as bacc
    from concourse.bass_utils import run_bass_kernel_spmd

    nc = bacc.Bacc("TRN2", target_bir_lowering=False, num_devices=1)
    arrays = {"in_" + k: np.ascontiguousarray(inputs[k]) for k in NAMES}
    arrays["in_consts"] = shape_constants(np)
    dram = {k[3:]: nc.dram_tensor(k, v.shape, F32, kind="ExternalInput").ap() for k, v in arrays.items()}
    out = nc.dram_tensor("out", (B, C, H, W), F32, kind="ExternalOutput").ap()
    build(nc, dram, out)
    r = run_bass_kernel_spmd(nc, [arrays], core_ids=[0])
    return r.results[0]["out"]
```

```python
from contextlib import ExitStack

import concourse.bass as bass
from concourse import mybir

F32 = mybir.dt.float32
BF16 = mybir.dt.bfloat16
U32 = mybir.dt.uint32
ALU = mybir.AluOpType
ACT = mybir.ActivationFunctionType
AX = mybir.AxisListType

P = 128
B, C, H, W = 4, 64, 16, 16
HW = H * W
BH = B // 2
TOK = P
NS = HW // TOK
NT = BH * NS * 2
NQ = BH * NS
K = 7
PAD = K // 2
GC = 16
G = C // GC
CR = C // 4
QUAD = 32
GPAIR = QUAD // GC
HP = H // 2
WINR = K + 1
TAP0 = 2 * W - 1
TAPS = TAP0 + P + 1
EDGES = [*range(PAD), *range(W - PAD, W)]
PARTS = [(1, 1), (1, 2), (1, 3), (2, 1), (2, 2), (3, 1)]
BIAS0 = CR * len(PARTS)
HEADS = 8
EXP = 8
FF = 128
TOPK = 2
CAPACITY = -(-B * HW * 5 // (4 * EXP))
EPS = 1e-5
BANK = 512
NBANK = 8
C_ID, C_REP, C_PAIR, C_BLK, C_MASK = 0, P, 2 * P, 3 * P, 4 * P
C_GROUP = C_MASK + 4
C_MEAN = C_GROUP + 2 * GPAIR
C_END = C_MEAN + 1
VPARTS, GPART = (slice(0, 2), slice(2, 5)), slice(5, HEADS)
WARM = {"start": 8, "stats": 3, "group": 1, "taps": 2, "reduced": 1, "bands": 4, "half": 1, "norm1": 1, "scores": 3,
        "softmax": 2, "wo": 4, "z": 2, "m": 2, "output": 2, "norm2": 1, "routing0": 6, "routing1": 6}

CHUNKS = [
    ("gn", "V"), ("w2T", "A"), ("w1T", "A"), ("wrep", "V"), ("bn", "A"), ("y0", "A"), ("y1", "A"), ("y2", "A"), ("y3", "A"),
    ("x0", "A"), ("x1", "A"), ("x2", "A"), ("x3", "A"),
    ("wpT", "A"),
    ("w0", "A"), ("w1", "A"), ("w2", "V"), ("w3", "A"), ("w4", "V"), ("w5", "A"), ("w6", "V"), ("w7", "A"),
    ("t0", "O"), ("t1", "O"), ("t2", "O"), ("t3", "O"), ("d0", "V"), ("d1", "V"), ("d2", "V"), ("d3", "V"),
    ("wvT", "A"), ("b1T", "A"),
    ("gram", "V"), ("eT", "A"), ("gk0", "V"), ("gk1", "A"), ("gks", "V"), ("attn0", "A"), ("attn1", "A"), ("astat", "V"),
    ("o0", "O"), ("o1", "O"), ("o2", "O"), ("z0", "V"), ("z1", "A"), ("z2", "V"), ("z3", "A"), ("m", "V"), ("o3", "O"),
    ("t2T", "A"), ("fT", "A"), ("fsum", "V"), ("logits", "V"),
    ("h0", "A"), ("h1", "A"), ("h2", "A"), ("h3", "A"), ("h4", "A"), ("h5", "A"),
    ("h6", "A"), ("h7", "A"), ("ffn0", "V"), ("ffn1", "V"), ("ffn2", "V"), ("ffn3", "V"), ("nT0", "V"), ("nT1", "V"),
]
INDEX = {name: j for j, (name, _) in enumerate(CHUNKS)}


FIRST = [(t, k, l) for t in range(BH) for k in range(TOPK) for l in range(2)]

E_ACT = [("product", 0), ("product", 1), ("read", 0), ("root", 0), ("product", 2), ("read", 1), ("apply", 0), ("root", 1),
         ("product", 3), ("read", 2), ("apply", 1), ("root", 2), ("read", 3), ("apply", 2), ("root", 3), ("apply", 3)]
E_DVE = [("product", 0), ("product", 1), ("stats", 0), ("moments", 0), ("product", 2), ("invert", 0), ("shift", 0), ("stats", 1),
         ("apply", 0), ("moments", 1), ("product", 3), ("invert", 1), ("shift", 1), ("stats", 2), ("apply", 1), ("moments", 2),
         ("invert", 2), ("shift", 2), ("stats", 3), ("apply", 2), ("moments", 3), ("invert", 3), ("shift", 3), ("apply", 3)]


def reads_until(j):
    return sum(1 for _, r in CHUNKS[:j + 1] if r == CHUNKS[j][1])


def build(nc, d, out):
    with ExitStack() as ctx:
        def sb(name, shape, dt=F32):
            return ctx.enter_context(nc.sbuf_tensor(name, shape, dt))

        def sem(name):
            return ctx.enter_context(nc.semaphore(name))

        consts = sb("consts", [P, C_END])
        ident = consts[:, C_ID:C_ID + P]
        rep = consts[:, C_REP:C_REP + P]
        pair = consts[:, C_PAIR:C_PAIR + P]
        blk = consts[:, C_BLK:C_BLK + P]
        mask = consts[:, C_MASK:C_MASK + 4]
        gmask = consts[:, C_GROUP:C_GROUP + 2 * GPAIR]
        meanw = consts[:, C_MEAN:C_MEAN + 1]
        ones = sb("ones", [P, P])
        eps = sb("eps", [P, 1])
        zeros = sb("zeros", [P, BANK], BF16)
        w1 = sb("w1", [CR, C])
        bnv = sb("bnv", [CR, 4])
        bn_ab = sb("bn_ab", [CR + 1, 2])
        bn_t = sb("bn_t", [CR, 4])
        w2l = sb("w2l", [K * K, G, CR + 1])
        w2T = sb("w2T", [CR + 1, G * K * K])
        w2a = sb("w2a", [P, G * K * K], BF16)
        w2r = sb("w2r", [P, G * K * K])
        w2b = sb("w2b", [P, G * K * K], BF16)
        w2c = sb("w2c", [P, G, K, K], BF16)
        wp = sb("wp", [C, C])
        wpT = sb("wpT", [P, C])
        wpg = sb("wpg", [P, GPAIR, 2, C])
        wq = sb("wq", [P, HEADS, 2, C])
        wk = sb("wk", [P, HEADS * C])
        wv = sb("wv", [C, HEADS * C])
        wvT = sb("wvT", [P, HEADS // 2, C])
        wo = sb("wo", [P, HEADS, C])
        wr = sb("wr", [P, 2, EXP])
        br = sb("br", [1, EXP])
        fw1 = sb("fw1", [P, EXP, FF])
        fw2 = sb("fw2", [P, EXP, C])
        fb1 = sb("fb1", [EXP, FF])
        fb1T = sb("fb1T", [P, EXP])
        fb2 = sb("fb2", [P, EXP, C])
        gb = sb("gb", [P, 2])
        x = sb("x", [P, BH, HW])
        xp = sb("xp", [P, BH, H + 2 * PAD, W])
        gst = sb("gst", [P, BH, 6])
        gmv = sb("gmv", [P, BH, 2])
        gd = sb("gd", [P, BH])
        gs = sb("gs", [P, BH, 2])
        gve = sb("gve", [P, BH])
        gn_t = sb("gn_t", [P, BH])
        gr = sb("gr", [P, BH])
        w1T = sb("w1T", [P, P])
        taps = sb("taps", [P, G, 1 + len(EDGES), TAPS], BF16)
        bns = sb("bns", [P, 2])
        yf = sb("yf", [P, W, 2, 2, BH * HP])
        ya = sb("ya", [P, W, 2, 2, BH * HP], BF16)
        yr = sb("yr", [P, W, 2, 2, BH * HP])
        yb = sb("yb", [P, W, 2, 2, BH * HP], BF16)
        yc = sb("yc", [P, W, 2, 2, BH * HP], BF16)
        xw = sb("xw", [P, BH, HP, P])
        wt = sb("wt", [P, 2, BH, HP, 2, G, W])
        dsb = sb("dsb", [P, GPAIR, BH, H, W])
        t = sb("t", [P, NT, C])
        e = sb("e", [P, NT, C])
        eT = sb("eT", [P, BH, HW])
        gram = sb("gram", [P, BH, P])
        gk = sb("gk", [P, BH, HEADS, C])
        a = sb("a", [P, HEADS, BH, C])
        ac = sb("ac", [P, HEADS, BH, C])
        asq = sb("asq", [P, HEADS, BH, C])
        amax = sb("amax", [P, HEADS, BH])
        ast = sb("ast", [P, 2, HEADS, BH])
        asc = sb("asc", [P, 2, HEADS, BH])
        wqs = sb("wqs", [P, HEADS])
        wks = sb("wks", [P, HEADS])
        ar = sb("ar", [P, HEADS, BH])
        prob = sb("prob", [P, HEADS, BH, C])
        rsum = sb("rsum", [P, HEADS, BH])
        wos = sb("wos", [P, HEADS, BH, C])
        z = sb("z", [P, 2, HEADS // 2, BH, C])
        m = sb("m", [P, BH, 2, C])
        t2 = sb("t2", [P, NT, C])
        t2T = sb("t2T", [P, BH, HW])
        f = sb("f", [P, NT, C])
        fT = sb("fT", [P, BH, HW])
        rl = sb("rl", [P, BH, 2, EXP])
        rt = sb("rt", [P, 2, B, EXP])
        rs = sb("rs", [P, 6, EXP])
        top = sb("top", [P, B, 8])
        topi = sb("topi", [P, B, 8], U32)
        pick = sb("pick", [P, B, TOPK], U32)
        gate = sb("gate", [P, B, TOPK])
        w1s = sb("w1s", [P, BH, TOPK, FF])
        w2s = sb("w2s", [P, B, TOPK, C])
        b2s = sb("b2s", [P, B, C])
        h = sb("h", [P, B, TOPK, HW])
        fb = sb("fb", [P, NT, C])
        u = sb("u", [P, NT, C])
        n = sb("n", [P, NT, C])
        res = sb("res", [P, BH, HW])
        norms = {k: (sb(k + "_st", [P, NT, 6]), sb(k + "_mv", [P, NT, 2]), sb(k + "_sd", [P, NT]), sb(k + "_nb", [P, NQ])) for k in "efn"}

        ps = ctx.enter_context(nc.psum_tensor("ps", [P, NBANK, BANK], F32))

        def bank(name):
            return ps[:, INDEX[name] % NBANK, :]

        written = sem("psum_written")
        read_v = sem("psum_read_by_vector")
        read_a = sem("psum_read_by_scalar")
        read_o = sem("psum_sums_read_by_scalar")
        v_seq = sem("vector_steps")
        dma = {k: sem("loaded_" + k) for k in ("const", "x", "w1", "var", "bn", "w2", "wp", "wq", "wk", "wv", "wo", "wr", "w_ffn", "fb1", "fb2", "gb", "br")}
        stored = sem("stored")
        const = {k: sem("made_" + k) for k in ("wq", "wr", "taps", "gram", "m", "xp", "wpg", "ones", "eps", "zeros")}
        made = {k: sem("done_" + k) for k in (
            "taps", "e", "wqs", "wks", "prob", "f", "gate", "w1s", "w2s", "b2s", "n", "bn_std", "e_g", "e_nb", "attn_in", "f_g", "n_g",
            "e_rs", "f_rs", "n_rs", "f_nb", "n_nb", "attn_out", "e_var", "e_std", "f_var", "f_std", "n_var", "n_std", "result",
            "tap_parts", "score_maxima", "scores_centred_g", "score_deviations_inverted", "scores_scaled_g", "row_sums_inverted",
            "wo_scaled_g", "residual_bias", "group_variances", "group_deviations", "reduction_rounded", "products_read_by_scalar",
            "gram_read_by_scalar", "scores_squared", "score_variances", "score_deviations", "scores_scaled_v", "m_read_by_scalar",
            "exp_first", "scaled_first_softmax", "exp_second", "gate_difference", "gate_exp", "choice", "channel_moments",
            "groupnorm_out", "bn_scale_shift", "reduction_parts", "wo_scaled_v", "score_sums")}
        block = ctx.enter_context(nc.Block())

        def wait_chunk(eng, name):
            eng.wait_ge(written, INDEX[name] + 1)

        def wait_read(eng, name):
            j = INDEX[name]
            eng.wait_ge({"V": read_v, "A": read_a, "O": read_o}[CHUNKS[j][1]], reads_until(j))

        def involution_reads(eng, copy, names, read):
            for name in names:
                wait_chunk(eng, name)
                src = bank(name)
                if name == "wpT":
                    copy(wpT[:, :], src[:, 0:C]).then_inc(read, 1)
                    continue
                i = int(name[1:])
                if name[0] == "x":
                    t_, q = divmod(4 * i, HP)
                    copy(xw[:, t_, q:q + 4, :], src).then_inc(read, 1)
                else:
                    g, w0 = i % G, 8 * (i // G)
                    copy(wt[:, :, :, :, :, g, w0:w0 + 8].rearrange("p l t q r w -> p (l t q) r w"),
                         src.rearrange("p (w r q) -> p q r w", w=8, r=2)).then_inc(read, 1)

        def read_product(eng, copy, i, quads, done):
            t_, s = divmod(i, NS)
            wait_chunk(eng, f"d{i}")
            for q in quads:
                r = slice(q * QUAD, (q + 1) * QUAD)
                g = q * GPAIR % G
                ins = copy(dsb[r, :, t_, 8 * s:8 * s + 8, :].rearrange("p g h w -> p h g w"),
                           bank(f"d{i}")[r, :].rearrange("p (h g w) -> p h g w", h=8, g=G)[:, :, g:g + GPAIR, :])
            ins.then_inc(done, 1)

        def edge_taps(copy, v, done):
            w = EDGES[v - 1]
            lo, hi = max(0, PAD - w), min(K, W + PAD - w)
            at = TAP0 - PAD
            dst = taps[:, :, v, at:at + K * W].rearrange("p g (i j) -> p g i j", j=W)[:, :, :, lo:hi]
            copy(dst, w2c[:, :, :, lo:hi]).then_inc(done, 1)

        @block.sync
        def _(sp):
            sp.dma_start(x[:, :, :], d["x"].rearrange("(t u) c h w -> (u c) t (h w)", t=BH)).then_inc(dma["x"], 16)
            sp.dma_start(w2l[:, :, 0:CR], d["L0_conv_w2"].rearrange("(g k) c -> k g c", g=G)).then_inc(dma["w2"], 16)
            sp.dma_start(w2l[:, :, CR:CR + 1], d["L0_conv_b2"].rearrange("(g k o) -> k g o", g=G, o=1), allow_slow_non_contiguous=True).then_inc(dma["w2"], 16)
            for name, i in ("var", 3), ("gamma", 0), ("mean", 2), ("beta", 1):
                sp.dma_start(bnv[:, i:i + 1], d["L0_conv_" + name].rearrange("(c o) -> c o", o=1)).then_inc(dma["var" if i == 3 else "bn"], 16)
            sp.dma_start(wp[:, :], d["L0_conv_wp"]).then_inc(dma["wp"], 16)
            for l in range(2):
                sp.dma_start(wk[l * C:(l + 1) * C, :], d["L1_attn_Wk"]).then_inc(dma["wk"], 16)
            sp.wait_ge(const["wq"], 1)
            for l in range(2):
                sp.dma_start(wq[l * C:(l + 1) * C, :, l, :], d["L1_attn_Wq"].rearrange("c (h e) -> c h e", h=HEADS)).then_inc(dma["wq"], 16)
            sp.dma_start(wv[:, :], d["L1_attn_Wv"]).then_inc(dma["wv"], 16)
            sp.dma_start(fb1[:, :], d["L1_ffn_b1"]).then_inc(dma["fb1"], 16)
            for l in range(2):
                sp.dma_start(wo[l * C:(l + 1) * C, :, :], d["L1_attn_Wo"].rearrange("(e h) j -> e h j", h=HEADS)).then_inc(dma["wo"], 16)
            for l in range(2):
                sp.dma_start(gb[l * C:(l + 1) * C, 0:1], d["L1_ffn_gamma"].rearrange("(c o) -> c o", o=1)).then_inc(dma["gb"], 16)
                sp.dma_start(gb[l * C:(l + 1) * C, 1:2], d["L1_ffn_beta"].rearrange("(c o) -> c o", o=1)).then_inc(dma["gb"], 16)
            for l in range(2):
                sp.dma_start(fw1[l * C:(l + 1) * C, :, :], d["L1_ffn_W1"].rearrange("e c f -> c e f")).then_inc(dma["w_ffn"], 16)
            sp.dma_start(fw2[:, :, :], d["L1_ffn_W2"].rearrange("e f j -> f e j")).then_inc(dma["w_ffn"], 16)
            for i in range(BH):
                sp.wait_ge(made["result"], i + 1)
                sp.dma_start(out.rearrange("(t u) c h w -> (u c) t (h w)", t=BH)[:, i, :], res[:, i, :]).then_inc(stored, 16)
            sp.wait_ge(stored, 16 * BH)

        @block.gpsimd
        def _(pool):
            def zero(ap, name):
                return pool.memset(ap, 0.0).then_inc(const[name], 1)

            zero(xp[:, :, 0:PAD, :], "xp")
            zero(xp[:, :, PAD + H:, :], "xp")
            zero(taps[:, 0:G // 2, :, :], "taps")
            zero(wr[:, :, :], "wr")
            zero(wq[:, :, :, :], "wq")
            pool.wait_ge(const["wr"], 1)
            for l in range(2):
                pool.dma_start(wr[l * C:(l + 1) * C, l, :], d["L1_ffn_Wr"]).then_inc(dma["wr"], 16)
            pool.dma_start(br[:, :], d["L1_ffn_br"].rearrange("(o e) -> o e", o=1)).then_inc(dma["br"], 16)
            pool.dma_start(fb2[:, :, :], d["L1_ffn_b2"].rearrange("(o e) j -> o e j", o=1).broadcast_to([P, EXP, C])).then_inc(dma["fb2"], 16)
            pool.wait_ge(made["tap_parts"], 1)
            pool.wait_ge(const["taps"], 2)
            for v in (1, 2):
                edge_taps(pool.tensor_copy, v, made["taps"])
            zero(gram[:, :, :], "gram")
            zero(m[:, :, :, :], "m")
            pool.wait_ge(dma["const"], 16)
            wait_read(pool, "wpT")
            pool.tensor_tensor(wpg[:, :, :, :].rearrange("p g l c -> p l g c"), wpT[:, :].unsqueeze(1).unsqueeze(1).to_broadcast([P, 2, GPAIR, C]),
                               gmask.rearrange("p (l g) -> p l g", l=2).unsqueeze(3).to_broadcast([P, 2, GPAIR, C]), ALU.mult).then_inc(const["wpg"], 1)

            def wide(v):
                return v.unsqueeze(3).to_broadcast([P, GPART.stop - GPART.start, BH, C])

            pool.wait_ge(made["score_maxima"], 2)
            pool.tensor_tensor(ac[:, GPART, :, :], a[:, GPART, :, :], wide(amax[:, GPART, :]), ALU.subtract).then_inc(made["scores_centred_g"], 1)
            pool.wait_ge(made["scores_centred_g"], 1)
            pool.wait_ge(made["score_deviations_inverted"], 1)
            pool.tensor_tensor(ac[:, GPART, :, :], ac[:, GPART, :, :], wide(ar[:, GPART, :]), ALU.mult).then_inc(made["scores_scaled_g"], 1)
            pool.wait_ge(made["row_sums_inverted"], len(VPARTS) + 1)
            pool.wait_ge(dma["wo"], 32)
            pool.tensor_tensor(wos[:, GPART, :, :], wo[:, GPART, :].unsqueeze(2).to_broadcast([P, GPART.stop - GPART.start, BH, C]),
                               wide(rsum[:, GPART, :]), ALU.mult).then_inc(made["wo_scaled_g"], 1)
            pool.wait_ge(made["f"], NQ)
            pool.wait_ge(made["f_g"], NQ)
            for i in range(BH):
                pool.wait_ge(made["b2s"], i + 1)
                pool.tensor_tensor(fb[:, 4 * i:4 * i + 4, :].rearrange("p (s l) c -> p s (l c)", s=NS), f[:, 4 * i:4 * i + 4, :].rearrange("p (s l) c -> p s (l c)", s=NS),
                                   b2s[:, 2 * i:2 * i + 2, :].rearrange("p l c -> p (l c)").unsqueeze(1).to_broadcast([P, NS, P]), ALU.add).then_inc(made["residual_bias"], 1)

        @block.scalar
        def _(act):
            act.dma_start(consts[:, :], d["consts"]).then_inc(dma["const"], 16)
            act.dma_start(w1[:, :], d["L0_conv_w1"]).then_inc(dma["w1"], 16)
            act.preload_act_table(ACT.Sqrt)

            def copy(dst, src):
                return act.activation(dst, src, ACT.Copy)

            def root(k, i):
                _, mv, sd, _ = norms[k]
                act.wait_ge(made[k + "_var"], i + 1)
                act.activation(sd[:, 2 * i:2 * i + 2], mv[:, 2 * i:2 * i + 2, 1], ACT.Sqrt, bias=eps[:, :]).then_inc(made[k + "_std"], 1)

            def apply(k, dst, src, i):
                _, _, sd, nb = norms[k]
                j = 2 * i + 1
                act.wait_ge(made[k + "_nb"], i + 1)
                act.activation(dst[:, j, :], src[:, j, :], ACT.Identity, scale=sd[:, j:j + 1], bias=nb[:, i:i + 1]).then_inc(made[k + "_g"], 1)

            def read_input(i):
                act.wait_ge(made["attn_in"], i + 1)
                copy(t[:, 2 * i:2 * i + 2, :], bank(f"t{i}")[:, 0:P]).then_inc(read_o, 1)

            def read_output(i):
                act.wait_ge(made["attn_out"], i + 1)
                copy(t2[:, 2 * i:2 * i + 2, :], bank(f"o{i}")[:, 0:P]).then_inc(read_o, 1)

            act.wait_ge(const["eps"], 1)
            act.wait_ge(dma["var"], 16)
            act.activation(bn_t[:, 0:1], bnv[:, 3:4], ACT.Sqrt, bias=eps[0:CR, :]).then_inc(made["bn_std"], 1)
            act.wait_ge(made["group_variances"], 1)
            act.activation(gr[:, :], gd[:, :], ACT.Sqrt, bias=eps[:, :]).then_inc(made["group_deviations"], 1)
            wait_chunk(act, "w2T")
            copy(w2T[:, :], bank("w2T")[0:CR + 1, 0:G * K * K]).then_inc(read_a, 1)
            wait_chunk(act, "w1T")
            copy(w1T[:, :], bank("w1T")[:, 0:P]).then_inc(read_a, 1)
            wait_chunk(act, "bn")
            copy(bns[:, :], bank("bn")[:, 0:2]).then_inc(read_a, 1)
            wait_read(act, "bn")
            for i in range(4):
                half, l = divmod(i, 2)
                wait_chunk(act, f"y{i}")
                ws = slice(W // 2 * half, W // 2 * (half + 1))
                act.activation(yf[:, ws, :, l, :], bank(f"y{i}")[:, 0:HW].rearrange("p (q r w) -> p w r q", r=2, w=W // 2), ACT.Relu,
                               bias=bns[:, 1:2], scale=bns[:, 0:1]).then_inc(read_a, 1)
            ws = slice(W // 2, W)
            wait_read(act, "y3")
            copy(ya[:, ws, :, :, :].rearrange("p w r l q -> p (w r l q)"), yf[:, ws, :, :, :].rearrange("p w r l q -> p (w r l q)")).then_inc(made["reduction_rounded"], 1)
            act.wait_ge(made["tap_parts"], 1)
            act.wait_ge(const["taps"], 2)
            for v in (3, 4):
                edge_taps(copy, v, made["taps"])
            involution_reads(act, copy, [c for c, r in CHUNKS[INDEX["x0"]:INDEX["w7"] + 1] if r == "A"], read_a)

            for step, i in E_ACT:
                if step == "product":
                    read_product(act, copy, i, (2, 3), made["products_read_by_scalar"])
                elif step == "read":
                    read_input(i)
                elif step == "root":
                    root("e", i)
                else:
                    apply("e", e, t, i)
            wait_chunk(act, "wvT")
            copy(wvT[:, :, :], bank("wvT")[:, 0:HEADS // 2 * C]).then_inc(read_a, 1)
            wait_chunk(act, "b1T")
            copy(fb1T[:, :], bank("b1T")[:, 0:EXP]).then_inc(read_a, 1)
            act.wait_ge(const["gram"], 1)
            wait_chunk(act, "gram")
            copy(gram[C:, :, C:], bank("gram")[C:, 0:BH * P].rearrange("p (t q) -> p t q", t=BH)[:, :, C:]).then_inc(made["gram_read_by_scalar"], 1)
            wait_chunk(act, "eT")
            copy(eT[:, :, :], bank("eT")).then_inc(read_a, 1)
            wait_chunk(act, "gk1")
            copy(gk[:, :, HEADS // 2:, :], bank("gk1").rearrange("p (t h e) -> p t h e", t=BH, h=HEADS // 2)).then_inc(read_a, 1)
            for i in range(2):
                hs = slice(i * HEADS // 2, (i + 1) * HEADS // 2)
                wait_chunk(act, f"attn{i}")
                act.activation(asq[:, hs, :, :], bank(f"attn{i}"), ACT.Square).then_inc(made["scores_squared"], 1)
            for i in range(2):
                hs = slice(i * HEADS // 2, (i + 1) * HEADS // 2)
                copy(a[:, hs, :, :], bank(f"attn{i}")).then_inc(read_a, 1)
            act.wait_ge(made["score_variances"], 1)
            act.activation(ar[:, :, :], asc[:, 1, :, :], ACT.Sqrt, bias=eps[:, :]).then_inc(made["score_deviations"], 1)
            act.preload_act_table(ACT.Exp)
            for j, part in enumerate(VPARTS):
                act.wait_ge(made["scores_scaled_v"], j + 1)
                act.activation(prob[:, part, :, :], ac[:, part, :, :], ACT.Exp).then_inc(made["prob"], 1)
            act.wait_ge(made["scores_scaled_g"], 1)
            act.activation(prob[:, GPART, :, :], ac[:, GPART, :, :], ACT.Exp).then_inc(made["prob"], 1)
            act.preload_act_table(ACT.Sqrt)
            for i in range(2):
                wait_chunk(act, f"z{2 * i + 1}")
                copy(z[:, 1, 2 * i:2 * i + 2, :, :], bank(f"z{2 * i + 1}")[:, 0:BANK // 2]).then_inc(read_a, 1)
            act.wait_ge(const["m"], 1)
            wait_chunk(act, "m")
            copy(m[C:, :, 1, :], bank("m")[C:, 0:BH * C].rearrange("p (t j) -> p t j", t=BH)).then_inc(made["m_read_by_scalar"], 1)
            for i in range(NQ):
                read_output(i)
            root("f", 0)
            root("f", 1)
            root("f", 2)
            apply("f", f, t2, 0)
            root("f", 3)
            apply("f", f, t2, 1)
            apply("f", f, t2, 2)
            apply("f", f, t2, 3)
            act.preload_act_table(ACT.Exp)
            act.wait_ge(dma["gb"], 64)
            wait_chunk(act, "t2T")
            act.activation(t2T[:, :, :], bank("t2T"), ACT.Identity, bias=gb[:, 1:2]).then_inc(read_a, 1)
            wait_chunk(act, "fT")
            copy(fT[:, :, :], bank("fT")).then_inc(read_a, 1)
            wait_read(act, "logits")
            act.activation(rt[:, 1, :, :], rt[:, 0, :, :], ACT.Exp).then_inc(made["exp_first"], 1)
            act.wait_ge(made["scaled_first_softmax"], 1)
            act.activation(rt[:, 1, :, :], rt[:, 0, :, :], ACT.Exp).then_inc(made["exp_second"], 1)
            act.wait_ge(made["gate_difference"], 1)
            act.activation(gate[:, :, 1:2], rs[:, 4, 0:B].unsqueeze(2), ACT.Exp).then_inc(made["gate_exp"], 1)
            act.preload_act_table(ACT.Gelu)
            act.wait_ge(made["choice"], 1)
            _, chosen = nc.values_load_multi_w_load_instructions(
                pick[0:1, :, :].rearrange("p b k -> p (b k)"), engines=[act.engine], min_val=0, max_val=EXP - 1,
                skip_runtime_bounds_check_because="pick keeps the low three bits only, so it is below EXP")
            act.wait_ge(read_a, reads_until(INDEX["b1T"]))
            for i, (t_, k, l) in enumerate(FIRST):
                b = 2 * t_ + l
                wait_chunk(act, f"h{i}")
                act.activation(h[:, b, k, :], bank(f"h{i}")[:, 0:HW], ACT.Gelu, bias=fb1T[:, bass.ds(chosen[TOPK * b + k], 1)]).then_inc(read_a, 1)
            act.preload_act_table(ACT.Sqrt)
            root("n", 0)
            root("n", 1)
            apply("n", n, u, 0)
            root("n", 2)
            apply("n", n, u, 1)
            root("n", 3)
            apply("n", n, u, 2)
            apply("n", n, u, 3)

        @block.vector
        def _(dve):
            steps = [0]

            def mark(ins):
                steps[0] += 1
                ins.then_inc(v_seq, 1)

            def after_mark():
                dve.wait_ge(v_seq, steps[0])

            def link(ins):
                mark(ins)
                after_mark()

            def newton(cases):
                for r, _, tmp in cases:
                    ins = dve.tensor_tensor(tmp, r, r, ALU.mult)
                link(ins)
                for _, v, tmp in cases:
                    ins = dve.scalar_tensor_tensor(tmp, tmp, -0.5, v, ALU.mult, ALU.mult)
                link(ins)
                for r, _, tmp in cases:
                    ins = dve.scalar_tensor_tensor(r, tmp, 1.5, r, ALU.add, ALU.mult)
                link(ins)

            counted = {}

            def stats(k, src, i):
                for j in (2 * i, 2 * i + 1):
                    ins = dve.bn_stats(norms[k][0][:, j, :], src[:, j, :])
                mark(ins)
                counted[k, i] = steps[0]

            def moments(k, i):
                st, mv, _, _ = norms[k]
                dve.wait_ge(v_seq, counted[k, i])
                dve.bn_aggr(mv[:, 2 * i, :], st[:, 2 * i, :])
                dve.bn_aggr(mv[:, 2 * i + 1, :], st[:, 2 * i + 1, :]).then_inc(made[k + "_var"], 1)

            def invert(k, i):
                sd = norms[k][2][:, 2 * i:2 * i + 2]
                dve.wait_ge(made[k + "_std"], i + 1)
                dve.reciprocal(sd, sd).then_inc(made[k + "_rs"], 1)

            def shift(k, i):
                _, mv, sd, nb = norms[k]
                j = 2 * i + 1
                dve.wait_ge(made[k + "_var"], i + 1)
                dve.wait_ge(made[k + "_rs"], i + 1)
                dve.scalar_tensor_tensor(nb[:, i:i + 1], mv[:, j, 0:1], -1.0, sd[:, j:j + 1], ALU.mult, ALU.mult).then_inc(made[k + "_nb"], 1)

            def apply(k, dst, src, i, tiles=1):
                _, mv, sd, _ = norms[k]
                dve.wait_ge(made[k + "_var"], i + 1)
                dve.wait_ge(made[k + "_rs"], i + 1)
                for j in range(2 * i, 2 * i + tiles):
                    ins = dve.tensor_scalar(dst[:, j, :], src[:, j, :], mv[:, j, 0:1], sd[:, j:j + 1], ALU.subtract, ALU.mult)
                ins.then_inc(made[k], 1)

            def add_output(i):
                dve.wait_ge(made["residual_bias"], i // NS + 1)
                wait_chunk(dve, f"ffn{i}")
                dve.tensor_tensor(u[:, 2 * i:2 * i + 2, :].rearrange("p i c -> p (i c)"), bank(f"ffn{i}")[:, 0:P],
                                  fb[:, 2 * i:2 * i + 2, :].rearrange("p i c -> p (i c)"), ALU.add).then_inc(read_v, 1)

            dve.memset(eps[:, :], EPS).then_inc(const["eps"], 1)
            dve.memset(zeros[:, :], 0.0).then_inc(const["zeros"], 1)
            dve.memset(ones[:, :], 1.0).then_inc(const["ones"], 1)
            dve.memset(bn_ab[:, 0:1], 0.0)
            link(dve.memset(bn_ab[:, 1:2], 1.0))
            dve.memset(taps[:, G // 2:, :, :], 0.0).then_inc(const["taps"], 1)
            dve.wait_ge(dma["x"], 16)
            for i in range(BH):
                ins = dve.bn_stats(gst[:, i, :], x[:, i, :])
            link(ins)
            for i in range(BH):
                ins = dve.bn_aggr(gmv[:, i, :], gst[:, i, :])
            ins.then_inc(made["channel_moments"], 1)
            dve.wait_ge(made["channel_moments"], 1)
            wait_chunk(dve, "gn")
            dve.tensor_copy(gs[:, :, :], bank("gn")[:, 0:2 * BH]).then_inc(read_v, 1)
            dve.wait_ge(read_v, reads_until(INDEX["gn"]))
            link(dve.tensor_tensor(gd[:, :], gmv[:, :, 0], gs[:, :, 0], ALU.subtract))
            link(dve.tensor_tensor(gd[:, :], gd[:, :], gd[:, :], ALU.mult))
            dve.tensor_tensor(gd[:, :], gd[:, :], gs[:, :, 1], ALU.add).then_inc(made["group_variances"], 1)
            dve.wait_ge(made["group_variances"], 1)
            dve.tensor_scalar(gve[:, :], gd[:, :], EPS, None, ALU.add)
            dve.wait_ge(dma["var"], 16)
            dve.tensor_scalar(bn_t[:, 3:4], bnv[:, 3:4], EPS, None, ALU.add)
            dve.wait_ge(made["bn_std"], 1)
            dve.reciprocal(bn_t[:, 1:2], bn_t[:, 0:1])
            dve.wait_ge(made["group_deviations"], 1)
            link(dve.reciprocal(gr[:, :], gr[:, :]))
            newton([(gr[:, :], gve[:, :], gn_t[:, :]), (bn_t[:, 1:2], bn_t[:, 3:4], bn_t[:, 2:3])])
            dve.wait_ge(dma["bn"], 48)
            mark(dve.tensor_tensor(bn_ab[0:CR, 0:1], bnv[:, 0:1], bn_t[:, 1:2], ALU.mult))
            for i in range(BH):
                dve.tensor_scalar(xp[:, i, PAD:PAD + H, :], x[:, i, :].rearrange("p (h w) -> p h w", h=H),
                                  gs[:, i, 0:1], gr[:, i:i + 1], ALU.subtract, ALU.mult).then_inc(made["groupnorm_out"], 1)
                after_mark()
                if i == 0:
                    mark(dve.tensor_tensor(bn_t[:, 2:3], bnv[:, 2:3], bn_ab[0:CR, 0:1], ALU.mult))
                else:
                    dve.tensor_tensor(bn_ab[0:CR, 1:2], bnv[:, 1:2], bn_t[:, 2:3], ALU.subtract).then_inc(made["bn_scale_shift"], 1)
            dve.wait_ge(dma["const"], 16)
            wait_chunk(dve, "wrep")
            src = bank("wrep")[:, 0:G * K * K]
            mark(dve.tensor_copy(w2a[:, :], src))
            after_mark()
            dve.scalar_tensor_tensor(w2r[:, :], w2a[:, :], mask[:, 2:3], src, ALU.mult, ALU.add).then_inc(read_v, 1)
            dve.wait_ge(read_v, reads_until(INDEX["wrep"]))
            link(dve.tensor_copy(w2b[:, :], w2r[:, :]))
            dve.scalar_tensor_tensor(w2c[:, :, :, :].rearrange("p g i j -> p (g i j)"), w2b[:, :], mask[:, 3:4], w2r[:, :], ALU.mult, ALU.add).then_inc(made["tap_parts"], 1)
            dve.wait_ge(made["tap_parts"], 1)
            dve.wait_ge(const["taps"], 2)
            at = TAP0 - PAD
            dve.tensor_copy(taps[:, :, 0, at:at + K * W].rearrange("p g (i j) -> p g i j", j=W)[:, :, :, 0:K], w2c[:, :, :, :]).then_inc(made["taps"], 1)
            for v in (5, 6):
                edge_taps(dve.tensor_copy, v, made["taps"])

            def split_y(half):
                ws = slice(8 * half, 8 * half + 8)
                def flat(v):
                    return v[:, ws, :, :, :].rearrange("p w r l q -> p (w r l q)")
                if half == 0:
                    wait_read(dve, "y1")
                    link(dve.tensor_copy(flat(ya), flat(yf)))
                else:
                    dve.wait_ge(made["reduction_rounded"], 1)
                link(dve.scalar_tensor_tensor(flat(yr), flat(ya), mask[:, 0:1], flat(yf), ALU.mult, ALU.add))
                link(dve.tensor_copy(flat(yb), flat(yr)))
                dve.scalar_tensor_tensor(flat(yc), flat(yb), mask[:, 1:2], flat(yr), ALU.mult, ALU.add).then_inc(made["reduction_parts"], 1)

            mine = [c for c, r in CHUNKS[INDEX["x0"]:INDEX["w7"] + 1] if r == "V"]
            split_y(0)
            split_y(1)
            involution_reads(dve, dve.tensor_copy, mine, read_v)
            dve.wait_ge(dma["wq"], 32)
            dve.wait_ge(dma["wk"], 32)
            dve.reduce_sum(wks[:, :], wk[:, :].rearrange("p (h e) -> p h e", h=HEADS), AX.X).then_inc(made["wks"], 1)
            for l in range(2):
                r = slice(l * C, (l + 1) * C)
                dve.reduce_sum(wqs[r, :], wq[r, :, l, :], AX.X).then_inc(made["wqs"], 1)

            for step, i in E_DVE:
                if step == "product":
                    read_product(dve, dve.tensor_copy, i, (0, 1), read_v)
                elif step == "stats":
                    wait_read(dve, f"t{i}")
                    stats("e", t, i)
                elif step == "moments":
                    moments("e", i)
                elif step == "invert":
                    invert("e", i)
                elif step == "shift":
                    shift("e", i)
                else:
                    apply("e", e, t, i)
            dve.wait_ge(const["gram"], 1)
            wait_chunk(dve, "gram")
            gr_ps = bank("gram")[:, 0:BH * P].rearrange("p (t q) -> p t q", t=BH)
            dve.tensor_copy(gram[0:C, :, 0:C], gr_ps[0:C, :, 0:C]).then_inc(read_v, 1)
            wait_chunk(dve, "gk0")
            dve.tensor_copy(gk[:, :, 0:HEADS // 2, :], bank("gk0").rearrange("p (t h e) -> p t h e", t=BH, h=HEADS // 2)).then_inc(read_v, 1)
            dve.wait_ge(made["wqs"], 2)
            wait_chunk(dve, "gks")
            dve.tensor_tensor(ast[:, 0, :, :], bank("gks")[:, 0:BH * HEADS].rearrange("p (t h) -> p h t", t=BH),
                              wqs[:, :].unsqueeze(2).to_broadcast([P, HEADS, BH]), ALU.mult).then_inc(read_v, 1)

            def wide(v, part):
                return v[:, part, :].unsqueeze(3).to_broadcast([P, part.stop - part.start, BH, C])

            def row_sums(part):
                return dve.reduce_sum(rsum[:, part, :], prob[:, part, :, :], AX.X)

            def invert_sums(part):
                dve.reciprocal(rsum[:, part, :], rsum[:, part, :]).then_inc(made["row_sums_inverted"], 1)

            def scale_wo(part):
                return dve.tensor_tensor(wos[:, part, :, :], wo[:, part, :].unsqueeze(2).to_broadcast([P, part.stop - part.start, BH, C]),
                                         wide(rsum, part), ALU.mult).then_inc(made["wo_scaled_v"], 1)

            for i in range(2):
                hs = slice(i * HEADS // 2, (i + 1) * HEADS // 2)
                dve.wait_ge(made["scores_squared"], i + 1)
                ins = dve.reduce_sum(ast[:, 1, hs, :], asq[:, hs, :, :], AX.X)
            ins.then_inc(made["score_sums"], 1)
            wait_read(dve, "attn0")
            dve.reduce_max(amax[:, 0:HEADS // 2, :], a[:, 0:HEADS // 2, :, :], AX.X).then_inc(made["score_maxima"], 1)
            wait_chunk(dve, "astat")
            dve.tensor_copy(asc[:, :, :, :], bank("astat")[:, 0:4 * HEADS]).then_inc(read_v, 1)
            dve.wait_ge(read_v, reads_until(INDEX["astat"]))
            mu, v = asc[:, 0, :, :].rearrange("p h t -> p (h t)"), asc[:, 1, :, :].rearrange("p h t -> p (h t)")
            link(dve.tensor_tensor(mu, mu, mu, ALU.mult))
            dve.tensor_tensor(v, v, mu, ALU.subtract).then_inc(made["score_variances"], 1)
            wait_read(dve, "attn1")
            dve.reduce_max(amax[:, HEADS // 2:, :], a[:, HEADS // 2:, :, :], AX.X).then_inc(made["score_maxima"], 1)
            dve.wait_ge(made["score_deviations"], 1)
            dve.reciprocal(ar[:, :, :], ar[:, :, :]).then_inc(made["score_deviations_inverted"], 1)
            dve.wait_ge(made["score_maxima"], 2)
            both = slice(0, GPART.start)
            link(dve.tensor_tensor(ac[:, both, :, :], a[:, both, :, :], wide(amax, both), ALU.subtract))
            dve.wait_ge(made["score_deviations_inverted"], 1)
            for part in VPARTS:
                dve.tensor_tensor(ac[:, part, :, :], ac[:, part, :, :], wide(ar, part), ALU.mult).then_inc(made["scores_scaled_v"], 1)
            dve.wait_ge(made["prob"], 1)
            link(row_sums(VPARTS[0]))
            invert_sums(VPARTS[0])
            dve.wait_ge(made["row_sums_inverted"], 1)
            dve.wait_ge(dma["wo"], 32)
            scale_wo(VPARTS[0])
            dve.wait_ge(made["prob"], 2)
            link(row_sums(VPARTS[1]))
            invert_sums(VPARTS[1])
            dve.wait_ge(made["prob"], 3)
            mark(row_sums(GPART))
            dve.wait_ge(made["row_sums_inverted"], 2)
            scale_wo(VPARTS[1])
            after_mark()
            invert_sums(GPART)
            for i in range(2):
                wait_chunk(dve, f"z{2 * i}")
                dve.tensor_copy(z[:, 0, 2 * i:2 * i + 2, :, :], bank(f"z{2 * i}")[:, 0:BANK // 2]).then_inc(read_v, 1)
            dve.wait_ge(const["m"], 1)
            wait_chunk(dve, "m")
            dve.tensor_copy(m[0:C, :, 0, :], bank("m")[0:C, 0:BH * C].rearrange("p (t j) -> p t j", t=BH)).then_inc(read_v, 1)
            for step, i in (stats, 0), (stats, 1), (moments, 0), (stats, 2), (moments, 1), (stats, 3), (invert, 0), (moments, 2), (shift, 0), \
                    (invert, 1), (moments, 3), (apply, 0), (shift, 1), (invert, 2), (apply, 1), (shift, 2), (invert, 3), (apply, 2), (shift, 3), (apply, 3):
                if step is stats:
                    wait_read(dve, f"o{i}")
                    stats("f", t2, i)
                elif step is apply:
                    apply("f", f, t2, i)
                else:
                    step("f", i)

            wait_chunk(dve, "fsum")
            dve.wait_ge(dma["wr"], 32)
            dve.tensor_tensor(rl[:, :, :, :].rearrange("p t l e -> p t (l e)"), wr[:, :, :].rearrange("p l e -> p (l e)").unsqueeze(1).to_broadcast([P, BH, 2 * EXP]),
                              bank("fsum")[:, 0:BH].unsqueeze(2).to_broadcast([P, BH, 2 * EXP]), ALU.mult).then_inc(read_v, 1)
            L, E = rt[:, 0, :, :], rt[:, 1, :, :]

            def over(v):
                return v.unsqueeze(2).to_broadcast([P, B, EXP])

            mx, sm, ld, sc = rs[:, 0, 0:B], rs[:, 1, 0:B], rs[:, 2, :], rs[:, 3, :]
            wait_chunk(dve, "logits")
            logits = bank("logits")[:, 0:B * EXP].rearrange("p (b e) -> p b e", b=B)
            link(dve.reduce_max(mx, logits, AX.X))
            dve.tensor_tensor(L, logits, over(mx), ALU.subtract).then_inc(read_v, 1)
            dve.wait_ge(made["exp_first"], 1)
            link(dve.reduce_sum(sm, E, AX.X))
            link(dve.reciprocal(sm, sm))
            link(dve.tensor_tensor(E, E, over(sm), ALU.mult))
            link(dve.reduce_sum(ld, E.rearrange("p b e -> p e b"), AX.X))
            link(dve.reciprocal(ld, ld))
            link(dve.tensor_scalar(sc, ld, float(CAPACITY) / HW, 1.0, ALU.mult, ALU.min))
            dve.tensor_tensor(L, E, sc.unsqueeze(1).to_broadcast([P, B, EXP]), ALU.mult).then_inc(made["scaled_first_softmax"], 1)
            dve.wait_ge(made["exp_second"], 1)
            for b in range(B):
                ins = dve.max(top[:, b, :], E[:, b, :])
            mark(ins)
            mark(dve.reduce_sum(sm, E, AX.X))
            after_mark()
            dve.reciprocal(sm, sm)
            dve.tensor_tensor(rs[:, 5, 0:B], top[:, :, 1], top[:, :, 0], ALU.subtract)
            for b in range(B):
                ins = dve.max_index(topi[:, b, :], top[:, b, :], E[:, b, :])
            link(ins)
            dve.tensor_scalar(pick[:, :, :], topi[:, :, 0:TOPK], EXP - 1, None, ALU.bitwise_and).then_inc(made["choice"], 1)
            dve.tensor_tensor(rs[:, 4, 0:B], rs[:, 5, 0:B], sm, ALU.mult).then_inc(made["gate_difference"], 1)
            dve.wait_ge(made["choice"], 1)
            _, chosen = nc.values_load_multi_w_load_instructions(
                pick[0:1, :, :].rearrange("p b k -> p (b k)"), engines=[dve.engine], min_val=0, max_val=EXP - 1,
                skip_runtime_bounds_check_because="pick keeps the low three bits only, so it is below EXP")
            chosen = [[chosen[TOPK * b + k] for k in range(TOPK)] for b in range(B)]
            dve.wait_ge(dma["w_ffn"], 48)
            for t_, k, l in FIRST:
                r = slice(l * C, (l + 1) * C)
                dve.tensor_copy(w1s[r, t_, k, :].unsqueeze(1), fw1[r, bass.ds(chosen[2 * t_ + l][k], 1), :]).then_inc(made["w1s"], 1)
            dve.wait_ge(made["gate_exp"], 1)
            link(dve.tensor_scalar(gate[:, :, 0], gate[:, :, 1], 1.0, None, ALU.add))
            link(dve.reciprocal(gate[:, :, 0], gate[:, :, 0]))
            dve.tensor_tensor(gate[:, :, 1], gate[:, :, 1], gate[:, :, 0], ALU.mult).then_inc(made["gate"], 1)
            dve.wait_ge(made["gate"], 1)
            dve.wait_ge(dma["fb2"], 16)
            for i in range(BH):
                bs = (2 * i, 2 * i + 1)
                for b in bs:
                    for k in range(TOPK):
                        dve.tensor_scalar(w2s[:, b, k, :].unsqueeze(1), fw2[:, bass.ds(chosen[b][k], 1), :], gate[:, b, k:k + 1], None, ALU.mult).then_inc(made["w2s"], 1)
                for b in bs:
                    ins = dve.tensor_scalar(b2s[:, b, :].unsqueeze(1), fb2[:, bass.ds(chosen[b][0], 1), :], gate[:, b, 0:1], None, ALU.mult)
                link(ins)
                for b in bs:
                    ins = dve.scalar_tensor_tensor(b2s[:, b, :].unsqueeze(1), fb2[:, bass.ds(chosen[b][1], 1), :], gate[:, b, 1:2], b2s[:, b, :].unsqueeze(1), ALU.mult, ALU.add)
                ins.then_inc(made["b2s"], 1)

            def result(i):
                wait_read(dve, "t2T")
                dve.wait_ge(dma["gb"], 64)
                wait_chunk(dve, f"nT{i}")
                dve.scalar_tensor_tensor(res[:, i, :], bank(f"nT{i}")[:, 0:HW], gb[:, 0:1], t2T[:, i, :], ALU.mult, ALU.add).then_inc(made["result"], 1)

            for step, i in (add_output, 0), (stats, 0), (add_output, 1), (moments, 0), (stats, 1), (add_output, 2), (moments, 1), (invert, 0), (stats, 2), \
                    (shift, 0), (invert, 1), (apply, 0), (add_output, 3), (moments, 2), (shift, 1), (stats, 3), (apply, 1), \
                    (invert, 2), (moments, 3), (shift, 2), (apply, 2), (invert, 3), (shift, 3), (apply, 3):
                if step is add_output:
                    add_output(i)
                elif step is stats:
                    wait_read(dve, f"ffn{i}")
                    stats("n", u, i)
                elif step is apply:
                    apply("n", n, u, i)
                else:
                    step("n", i)
            for i in range(BH):
                result(i)

        @block.tensor
        def _(pe):
            def begin(name):
                j = INDEX[name]
                if j >= NBANK:
                    wait_read(pe, CHUNKS[j - NBANK][0])
                return bank(name)

            def mm(dst, lhsT, rhs, start=True, stop=True):
                return pe.matmul(dst, lhsT, rhs, start=start, stop=stop)

            def keep_warm(name, n):
                dst = begin(name)
                for _ in range(n):
                    mm(dst, zeros[:, 0:P], zeros[:, :])

            pe.wait_ge(const["zeros"], 1)
            keep_warm("gn", WARM["start"])
            dst = begin("gn")
            pe.wait_ge(dma["const"], 16)
            pe.wait_ge(made["channel_moments"], 1)
            mm(dst[:, 0:2 * BH], pair, gmv[:, :, :]).then_inc(written, 1)
            keep_warm("w2T", WARM["stats"])
            dst = begin("w2T")
            pe.wait_ge(dma["w2"], 32)
            for g in range(G):
                ins = mm(dst[0:CR + 1, g * K * K:(g + 1) * K * K], w2l[:, g, :], ident[0:K * K, 0:K * K])
            ins.then_inc(written, 1)
            dst = begin("w1T")
            pe.wait_ge(dma["w1"], 16)
            pe.wait_ge(dma["const"], 16)
            for l in range(2):
                ins = mm(dst[l * C:(l + 1) * C, 0:P], w1[:, :], rep[0:CR, :])
            ins.then_inc(written, 1)
            keep_warm("wrep", WARM["group"])
            dst = begin("wrep")
            wait_read(pe, "w2T")
            mm(dst[:, 0:G * K * K], rep[0:CR + 1, :], w2T[:, :]).then_inc(written, 1)
            keep_warm("bn", WARM["taps"])
            wait_read(pe, "w1T")
            dst = begin("bn")
            pe.wait_ge(made["bn_scale_shift"], 1)
            mm(dst[:, 0:2], rep[0:CR + 1, :], bn_ab[:, :]).then_inc(written, 1)
            pe.wait_ge(made["groupnorm_out"], BH)
            for i in range(4):
                half, l = divmod(i, 2)
                r = slice(l * C, (l + 1) * C)
                mm(begin(f"y{i}")[:, 0:HW], w1T[r, :], xp[r, :, PAD:PAD + H, W // 2 * half:W // 2 * (half + 1)]).then_inc(written, 1)
            keep_warm("x0", WARM["reduced"])
            pe.wait_ge(const["xp"], 2)
            for i in range(4):
                dst = begin(f"x{i}")
                for j in range(4):
                    t_, q = divmod(4 * i + j, HP)
                    ins = pe.transpose(dst[:, j * P:(j + 1) * P], xp[:, t_, 2 * q:2 * q + WINR, :], ident)
                ins.then_inc(written, 1)
            dst = begin("wpT")
            pe.wait_ge(dma["wp"], 16)
            for l in range(2):
                ins = mm(dst[l * C:(l + 1) * C, 0:C], wp[:, :], ident[0:C, 0:C])
            ins.then_inc(written, 1)
            keep_warm("w0", WARM["bands"])
            pe.wait_ge(made["taps"], 1 + len(EDGES))
            for half in range(2):
                if half == 1:
                    keep_warm("w4", WARM["half"])
                pe.wait_ge(made["reduction_parts"], half + 1)
                dsts = [begin(f"w{G * half + g}") for g in range(G)]
                for g in range(G):
                    for w in range(8 * half, 8 * half + 8):
                        v = EDGES.index(w) + 1 if w in EDGES else 0
                        for r in range(2):
                            at = TAP0 - W * r - w
                            c0 = ((w - 8 * half) * 2 + r) * 2 * BH * HP
                            ins = mm(dsts[g][:, c0:c0 + 2 * BH * HP], taps[:, g, v, at:at + P], yc[:, w, r, :, :])
                    ins.then_inc(written, 1)
            for i in range(NQ):
                t_, s = divmod(i, NS)
                mm(begin(f"t{i}")[:, 0:P], x[:, t_, s * TOK:(s + 1) * TOK], ident, True, False).then_inc(written, 1)
            wait_read(pe, "w6")
            wait_read(pe, "w7")

            def group_product(i):
                t_, s = divmod(i, NS)
                dst = begin(f"d{i}")
                for j in range(4):
                    q = 4 * s + j
                    for l in range(2):
                        ins = mm(dst[l * C:(l + 1) * C, j * P:(j + 1) * P], xw[:, t_, q, l * C:(l + 1) * C], wt[:, l, t_, q, :, :, :])
                ins.then_inc(written, 1)

            def project(i):
                t_, s = divmod(i, NS)
                wait_read(pe, f"d{i}")
                pe.wait_ge(made["products_read_by_scalar"], i + 1)
                for g in range(GPAIR):
                    ins = mm(bank(f"t{i}")[:, 0:P], dsb[:, g, t_, 8 * s:8 * s + 8, :], wpg[:, g, :, :], False, g == GPAIR - 1)
                ins.then_inc(made["attn_in"], 1)

            group_product(0)
            pe.wait_ge(const["wpg"], 1)
            for i in range(1, NQ):
                group_product(i)
                project(i - 1)
            project(NQ - 1)
            dst = begin("wvT")
            pe.wait_ge(dma["wv"], 16)
            for i in range(HEADS // 2):
                ins = pe.transpose(dst[:, i * C:(i + 1) * C], wv[:, i * P:(i + 1) * P], ident[0:C, 0:C])
            ins.then_inc(written, 1)
            dst = begin("b1T")
            pe.wait_ge(dma["fb1"], 16)
            pe.transpose(dst[:, 0:EXP], fb1[:, :], ident[0:EXP, 0:EXP]).then_inc(written, 1)
            gram_, eT_ = begin("gram"), begin("eT")
            for i in range(NQ):
                t_, s = divmod(i, NS)
                pe.wait_ge(made["e"], i + 1)
                pe.wait_ge(made["e_g"], i + 1)
                last = mm(gram_[:, t_ * P:(t_ + 1) * P], e[:, 2 * i:2 * i + 2, :], e[:, 2 * i:2 * i + 2, :], s == 0, s == NS - 1)
                if i == NQ - 1:
                    last.then_inc(written, 1)
                ins = pe.transpose(eT_[:, i * P:(i + 1) * P], e[:, 2 * i:2 * i + 2, :], ident)
                if i == NQ - 1:
                    ins.then_inc(written, 1)
                if i < NQ - 2:
                    keep_warm("gk0", WARM["norm1"])
            pe.wait_ge(dma["wk"], 32)
            wait_read(pe, "gram")
            pe.wait_ge(made["gram_read_by_scalar"], 1)
            for i in range(2):
                dst = begin(f"gk{i}")
                for t_ in range(BH):
                    ins = mm(dst[:, t_ * HEADS // 2 * C:(t_ + 1) * HEADS // 2 * C], gram[:, t_, :], wk[:, i * HEADS // 2 * C:(i + 1) * HEADS // 2 * C])
                ins.then_inc(written, 1)
            dst = begin("gks")
            pe.wait_ge(made["wks"], 1)
            for t_ in range(BH):
                ins = mm(dst[:, t_ * HEADS:(t_ + 1) * HEADS], gram[:, t_, :], wks[:, :])
            ins.then_inc(written, 1)
            pe.wait_ge(dma["wq"], 32)
            for i in range(2):
                wait_read(pe, f"gk{i}")
                dst = begin(f"attn{i}")
                for q in range(HEADS // 2):
                    hd = i * HEADS // 2 + q
                    ins = mm(dst[:, q * P:(q + 1) * P], wq[:, hd, :, :], gk[:, :, hd, :])
                ins.then_inc(written, 1)
            for i in range(2):
                pe.wait_ge(made["scores_squared"], i + 1)
                keep_warm("astat", WARM["scores"])
            dst = begin("astat")
            pe.wait_ge(made["score_sums"], 1)
            mm(dst[:, 0:4 * HEADS], blk, ast[:, :, :, :]).then_inc(written, 1)
            wait_read(pe, "t3")
            for i, (name, count) in enumerate((("score_variances", 1), ("score_deviations_inverted", 1), ("prob", 1))):
                pe.wait_ge(made[name], count)
                mm(begin(f"o{i}")[:, 0:P], ident, t[:, 2 * i:2 * i + 2, :], True, False).then_inc(written, 1)
                keep_warm("z0", WARM["softmax"])
            dsts = [begin(f"z{j}") for j in range(4)]
            for hd in range(HEADS):
                if hd == VPARTS[1].start:
                    keep_warm("m", WARM["wo"])
                for j, part in enumerate(VPARTS):
                    if hd == part.start:
                        pe.wait_ge(made["wo_scaled_v"], j + 1)
                if hd == GPART.start:
                    pe.wait_ge(made["wo_scaled_g"], 1)
                for l in range(2):
                    r = slice(l * C, (l + 1) * C)
                    for t_ in range(BH):
                        c0 = (hd % 4 // 2 * BH + t_) * C
                        o = slice(hd % 2 * C, hd % 2 * C + C)
                        ins = mm(dsts[hd // 4 * 2 + l][o, c0:c0 + C], prob[r, hd, t_, :], wos[r, hd, t_, :])
                    if hd % 4 == 3:
                        ins.then_inc(written, 1)
            keep_warm("m", WARM["z"])
            wait_read(pe, "wvT")
            dst = begin("m")
            for i in range(HEADS // 2):
                if i % 2 == 0:
                    wait_read(pe, f"z{i}")
                    wait_read(pe, f"z{i + 1}")
                for l in range(2):
                    ins = mm(dst[l * C:(l + 1) * C, 0:BH * C], wvT[:, i, :], z[:, l, i, :, :], i == 0, i == HEADS // 2 - 1)
            ins.then_inc(written, 1)
            keep_warm("fsum", WARM["m"])
            wait_read(pe, "eT")
            wait_read(pe, "m")
            pe.wait_ge(made["m_read_by_scalar"], 1)
            for i in range(NQ):
                t_, s = divmod(i, NS)
                if i == NQ - 1:
                    mm(begin(f"o{i}")[:, 0:P], ident, t[:, 2 * i:2 * i + 2, :], True, False).then_inc(written, 1)
                mm(bank(f"o{i}")[:, 0:P], eT[:, t_, s * TOK:(s + 1) * TOK], m[:, t_, :, :], False, True).then_inc(made["attn_out"], 1)
            dst = begin("t2T")
            for i in range(NQ):
                wait_read(pe, f"o{i}")
                ins = pe.transpose(dst[:, i * P:(i + 1) * P], t2[:, 2 * i:2 * i + 2, :], ident)
                if i == NQ - 1:
                    ins.then_inc(written, 1)
                keep_warm("fsum", WARM["output"])
            fT_, fsum_ = begin("fT"), begin("fsum")
            for i in range(NQ):
                t_, s = divmod(i, NS)
                pe.wait_ge(made["f"], i + 1)
                pe.wait_ge(made["f_g"], i + 1)
                last = pe.transpose(fT_[:, i * P:(i + 1) * P], f[:, 2 * i:2 * i + 2, :], ident)
                if i == NQ - 1:
                    last.then_inc(written, 1)
                ins = mm(fsum_[:, t_:t_ + 1], f[:, 2 * i:2 * i + 2, :], meanw, s == 0, s == NS - 1)
                if i == NQ - 1:
                    ins.then_inc(written, 1)
                else:
                    keep_warm("logits", WARM["norm2"])
            dst = begin("logits")[:, 0:B * EXP]
            pe.wait_ge(const["ones"], 1)
            pe.wait_ge(dma["br"], 16)
            mm(dst, ones[0:1, :], br[:, :].unsqueeze(1).to_broadcast([1, B, EXP]), True, False)
            wait_read(pe, "fsum")
            mm(dst, ones[:, :], rl[:, :, :, :], False, True).then_inc(written, 1)
            for i in range(2):
                pe.wait_ge(made[("exp_first", "scaled_first_softmax")[i]], 1)
                keep_warm("h0", WARM["routing%d" % i])

            wait_read(pe, "fT")
            for i, (t_, k, l) in enumerate(FIRST):
                r = slice(l * C, (l + 1) * C)
                pe.wait_ge(made["w1s"], i + 1)
                mm(begin(f"h{i}")[:, 0:HW], w1s[r, t_, k, :], fT[r, t_, :]).then_inc(written, 1)
            for i in range(NQ):
                t_, s = divmod(i, NS)
                dst = begin(f"ffn{i}")
                wait_read(pe, f"h{4 * t_ + 3}")
                pe.wait_ge(made["w2s"], 4 * (t_ + 1))
                for l in range(2):
                    b = 2 * t_ + l
                    for k in range(TOPK):
                        ins = mm(dst[:, l * C:(l + 1) * C], h[:, b, k, s * TOK:(s + 1) * TOK], w2s[:, b, k, :], k == 0, k == TOPK - 1)
                ins.then_inc(written, 1)
            for i in range(BH):
                dst = begin(f"nT{i}")
                for s in range(NS):
                    j = NS * i + s
                    pe.wait_ge(made["n"], j + 1)
                    pe.wait_ge(made["n_g"], j + 1)
                    ins = pe.transpose(dst[:, s * P:(s + 1) * P], n[:, 2 * j:2 * j + 2, :], ident)
                ins.then_inc(written, 1)


NAMES = ["x", "L0_conv_w1", "L0_conv_gamma", "L0_conv_beta", "L0_conv_mean", "L0_conv_var", "L0_conv_w2", "L0_conv_b2",
         "L0_conv_wp", "L1_attn_Wq", "L1_attn_Wk", "L1_attn_Wv", "L1_attn_Wo", "L1_ffn_Wr", "L1_ffn_br", "L1_ffn_W1",
         "L1_ffn_b1", "L1_ffn_W2", "L1_ffn_b2", "L1_ffn_gamma", "L1_ffn_beta"]


def shape_constants(np):
    c = np.zeros((P, C_END), np.float32)
    p = np.arange(P)
    c[:, C_ID:C_ID + P] = np.eye(P)
    for i in range(len(PARTS)):
        c[0:CR, C_REP + CR * i:C_REP + CR * (i + 1)] = np.eye(CR)
    c[CR, C_REP + BIAS0:C_REP + BIAS0 + 3] = 1.0
    c[:, C_PAIR:C_PAIR + P] = (p[:, None] // 2 == p[None, :] // 2) * 0.5
    c[:, C_BLK:C_BLK + P] = (p[:, None] // C == p[None, :] // C) / (C * C)
    parts = [q for q in PARTS for _ in range(CR)] + [(1, 1), (1, 2), (1, 3)]
    for row, (yp, wp_) in enumerate(parts):
        c[row, C_MASK:C_MASK + 4] = [-(yp > 1), -(yp > 2), -(wp_ > 1), -(wp_ > 2)]
    c[:, C_GROUP:C_GROUP + 2 * GPAIR] = p[:, None] // C * GPAIR + p[:, None] // GC % GPAIR == np.arange(2 * GPAIR)[None, :]
    c[:, C_MEAN] = 1.0 / HW
    return c


def kernel(**inputs):
    import numpy as np
    import concourse.bacc as bacc
    from concourse.bass_utils import run_bass_kernel_spmd

    nc = bacc.Bacc("TRN2", target_bir_lowering=False, num_devices=1)
    arrays = {"in_" + k: np.ascontiguousarray(inputs[k]) for k in NAMES}
    arrays["in_consts"] = shape_constants(np)
    dram = {k[3:]: nc.dram_tensor(k, v.shape, F32, kind="ExternalInput").ap() for k, v in arrays.items()}
    out = nc.dram_tensor("out", (B, C, H, W), F32, kind="ExternalOutput").ap()
    build(nc, dram, out)
    r = run_bass_kernel_spmd(nc, [arrays], core_ids=[0])
    return r.results[0]["out"]
```
